# Optimizing a Trainium2 kernel written in Bass

```python
import numpy as np
import jax
import jax.numpy as jnp

def _softmax(x, axis=-1):
    return jax.nn.softmax(x, axis=axis)

def _gelu(x):
    return jax.nn.gelu(x, approximate=True)

def _silu(x):
    return jax.nn.silu(x)

def _sigmoid(x):
    return jax.nn.sigmoid(x)

def _layernorm(x, axis=-1, eps=1e-05):
    m = jnp.mean(x, axis=axis, keepdims=True)
    v = jnp.var(x, axis=axis, keepdims=True)
    return (x - m) / jnp.sqrt(v + eps)

def _scatter_add(tgt, idx, src, axis=0):
    return tgt.at[idx].add(src)

def _segment_sum(src, seg, n):
    return jax.ops.segment_sum(src, seg, n)
kernel_name = 'mk_flamingo_gated_d1_seqx_r4_5b3756'

def setup_inputs(seed: int=0):
    np.random.seed(seed)
    _w = jnp.asarray

    def _rec_inputs():
        import jax
        import jax.numpy as jnp
        _rk = jax.random.key(seed)
        x = 0.0001212 + 1 * jax.random.normal(jax.random.fold_in(_rk, 1), (8, 256, 1024), jnp.float32)
        _lenS = 256 - jax.random.randint(jax.random.fold_in(_rk, 7), (8,), 0, max(1, 256 // 4) + 1, jnp.int32)
        _lenS2 = 256 - jax.random.randint(jax.random.fold_in(_rk, 8), (8,), 0, max(1, 256 // 4) + 1, jnp.int32)
        _ctx_4096P = jax.random.normal(jax.random.fold_in(_rk, 11), (8, 16, 1024), jnp.float32)
        _ctx_4096c = jax.random.dirichlet(jax.random.fold_in(_rk, 511), 0.3 * jnp.ones((16,), jnp.float32), (8, 256))
        _ctx_4096t = jnp.einsum('bsk,bkd->bsd', _ctx_4096c, _ctx_4096P)
        _ctx_4096t = _ctx_4096t * jax.lax.rsqrt(jnp.mean(jnp.square(_ctx_4096t)) + 1e-12) * 0.953939
        ctx_4096 = -0.000125008 + 0.999885 * (_ctx_4096t + 0.3 * jax.random.normal(jax.random.fold_in(_rk, 611), (8, 256, 1024), jnp.float32))
        _g = jax.random.normal(jax.random.fold_in(_rk, 9001), (2, 1), jnp.float32)
        _g = jnp.sign(_g) * jnp.maximum(jnp.abs(_g), 1.0) + (_g == 0) * 1.0
        g_xattn = _g[0]
        g_ffn = _g[1]
        return (x, ctx_4096, g_xattn, g_ffn)
    x, ctx_4096, g_xattn, g_ffn = _rec_inputs()

    def _L0_xattn_setup():
        import jax, jax.numpy as jnp
        import numpy as np
        N, C, S = (16, 128, 1024)
        rng = jax.random.key(seed)
        k1, k2, k3 = jax.random.split(rng, 3)
        return {'key': jax.random.normal(k1, (N, C, S), dtype=jnp.float32), 'value': jax.random.normal(k2, (N, C, S), dtype=jnp.float32), 'query': jax.random.normal(k3, (N, C, S), dtype=jnp.float32)}
    _L0_xattn_all = _L0_xattn_setup()
    _L0_xattn_in = {k: v for k, v in _L0_xattn_all.items() if k in ()}
    del _L0_xattn_all

    def _L0_ffn_setup():
        import jax, jax.numpy as jnp
        import numpy as np
        _FP8_MAX = 448.0

        def _quantize_fp8(w):
            scale = jnp.maximum(jnp.max(jnp.abs(w)).astype(jnp.float32) / _FP8_MAX, 1e-12)
            w_q = (w / scale).astype(jnp.float8_e4m3fn).astype(jnp.float32)
            return (w_q, scale)

        def _fake_quant_fp8_linear(x, w_q, in_scale, w_scale):
            x_q = jnp.clip(x / in_scale, -_FP8_MAX, _FP8_MAX)
            x_dq = x_q.astype(jnp.float8_e4m3fn).astype(jnp.float32) * in_scale
            w_dq = w_q * w_scale
            return jnp.einsum('bsh,ih->bsi', x_dq, w_dq)
        key = jax.random.key(seed)
        k_x, k_g, k_u, k_d = jax.random.split(key, 4)
        B, S, H, I = (4, 512, 1024, 2752)
        x = jax.random.normal(k_x, (B, S, H), dtype=jnp.float32)
        gate = jax.random.normal(k_g, (I, H), dtype=jnp.float32) * 0.05
        up = jax.random.normal(k_u, (I, H), dtype=jnp.float32) * 0.05
        down = jax.random.normal(k_d, (H, I), dtype=jnp.float32) * 0.05
        gate_w, gate_w_scale = _quantize_fp8(gate)
        up_w, up_w_scale = _quantize_fp8(up)
        down_w, down_w_scale = _quantize_fp8(down)
        one = jnp.float32(1.0)
        return {'x': x, 'gate_w': gate_w, 'up_w': up_w, 'down_w': down_w, 'gate_w_scale': gate_w_scale, 'up_w_scale': up_w_scale, 'down_w_scale': down_w_scale, 'gate_in_scale': one, 'up_in_scale': one, 'down_in_scale': one}
    _L0_ffn_all = _L0_ffn_setup()
    _L0_ffn_in = {k: v for k, v in _L0_ffn_all.items() if k in ('gate_w', 'up_w', 'down_w', 'gate_w_scale', 'up_w_scale', 'down_w_scale', 'gate_in_scale', 'up_in_scale', 'down_in_scale')}
    del _L0_ffn_all
    return {'x': x, 'ctx_4096': ctx_4096, 'g_xattn': g_xattn, 'g_ffn': g_ffn, 'L0_ffn_gate_w': _L0_ffn_in['gate_w'], 'L0_ffn_up_w': _L0_ffn_in['up_w'], 'L0_ffn_down_w': _L0_ffn_in['down_w'], 'L0_ffn_gate_w_scale': _L0_ffn_in['gate_w_scale'], 'L0_ffn_up_w_scale': _L0_ffn_in['up_w_scale'], 'L0_ffn_down_w_scale': _L0_ffn_in['down_w_scale'], 'L0_ffn_gate_in_scale': _L0_ffn_in['gate_in_scale'], 'L0_ffn_up_in_scale': _L0_ffn_in['up_in_scale'], 'L0_ffn_down_in_scale': _L0_ffn_in['down_in_scale']}

def reference(x, ctx_4096, g_xattn, g_ffn, L0_ffn_gate_w, L0_ffn_up_w, L0_ffn_down_w, L0_ffn_gate_w_scale, L0_ffn_up_w_scale, L0_ffn_down_w_scale, L0_ffn_gate_in_scale, L0_ffn_up_in_scale, L0_ffn_down_in_scale):
    import jax
    import jax.numpy as jnp

    def _L0_xattn_ref(key, value, query):
        import jax, jax.numpy as jnp
        import numpy as np
        N, C, S = (16, 128, 1024)
        KC = key.shape[1]
        sim = jnp.einsum('ncs,nds->ncd', key, query) * KC ** (-0.5)
        sim = jax.nn.softmax(sim, axis=1)
        context = jnp.einsum('ncd,nds->ncs', sim, value)
        return context

    def _L0_ffn_ref(x, gate_w, up_w, down_w, gate_w_scale, up_w_scale, down_w_scale, gate_in_scale, up_in_scale, down_in_scale):
        import jax, jax.numpy as jnp
        import numpy as np
        _FP8_MAX = 448.0

        def _quantize_fp8(w):
            scale = jnp.maximum(jnp.max(jnp.abs(w)).astype(jnp.float32) / _FP8_MAX, 1e-12)
            w_q = (w / scale).astype(jnp.float8_e4m3fn).astype(jnp.float32)
            return (w_q, scale)

        def _fake_quant_fp8_linear(x, w_q, in_scale, w_scale):
            x_q = jnp.clip(x / in_scale, -_FP8_MAX, _FP8_MAX)
            x_dq = x_q.astype(jnp.float8_e4m3fn).astype(jnp.float32) * in_scale
            w_dq = w_q * w_scale
            return jnp.einsum('bsh,ih->bsi', x_dq, w_dq)
        gate_out = _fake_quant_fp8_linear(x, gate_w, gate_in_scale, gate_w_scale)
        up_out = _fake_quant_fp8_linear(x, up_w, up_in_scale, up_w_scale)
        hidden = jax.nn.silu(gate_out) * up_out
        return _fake_quant_fp8_linear(hidden, down_w, down_in_scale, down_w_scale)
    x = x + jnp.tanh(g_xattn[0]) * _L0_xattn_ref(ctx_4096, ctx_4096, _layernorm(x, axis=-1))
    x = x + jnp.tanh(g_ffn[0]) * _L0_ffn_ref(_layernorm(x, axis=-1), L0_ffn_gate_w, L0_ffn_up_w, L0_ffn_down_w, L0_ffn_gate_w_scale, L0_ffn_up_w_scale, L0_ffn_down_w_scale, L0_ffn_gate_in_scale, L0_ffn_up_in_scale, L0_ffn_down_in_scale)
    return x

_drawn_inputs = setup_inputs


def setup_inputs(seed=0):
    import zlib

    import numpy as np

    out = dict(_drawn_inputs(seed))
    spreads = {}
    factors = {}
    for name, (base, spread) in spreads.items():
        noise = np.random.default_rng([zlib.crc32(name.encode()), seed]).standard_normal(out[name].shape)
        drawn = base * np.exp(spread * noise) if base else spread * noise
        out[name] = jnp.asarray(drawn.astype(out[name].dtype))
    for name, factor in factors.items():
        out[name] = (out[name] * factor).astype(out[name].dtype)
    return out
```

```python
from contextlib import ExitStack

import concourse.bass as bass
from concourse import mybir

P = 128
BATCH, SEQ, DIM, INNER = 8, 256, 1024, 2752
TT = SEQ // P
KD = DIM // P
HALVES = DIM // 512
PAIRS = -(-INNER // 256)
KI = 2 * PAIRS
TAIL = INNER - (PAIRS - 1) * 256
DTAIL = INNER - (KI - 1) * P
FULL = PAIRS - 1
EPS = 1e-5
FP8_MAX = 448.0
MIN_NORMAL = 2.0 ** -6
ROUND = 2.0 ** 20
SCORE_SCALE = float(SEQ) ** -0.5


def gated_xattn_ffn(nc, x, ctx, ctx_t, scalars, gate_main, gate_tail, up_main, up_tail,
                    down_main, down_tail, out):
    f32, bf16, u16 = mybir.dt.float32, mybir.dt.bfloat16, mybir.dt.uint16
    ALU, ACT, AX = mybir.AluOpType, mybir.ActivationFunctionType, mybir.AxisListType

    es = ExitStack()
    with es:
        def sb(name, shape, dt):
            return es.enter_context(nc.sbuf_tensor(name, shape, dt))

        def ps(name):
            return es.enter_context(nc.psum_tensor(name, [P, 512], f32))

        def sem(name):
            return es.enter_context(nc.semaphore(name))

        w_gate = sb("w_gate", [P, PAIRS, KD, 256], bf16)
        w_up = sb("w_up", [P, PAIRS, KD, 256], bf16)
        w_down = sb("w_down", [P, KI, DIM], bf16)
        hq = sb("hq", [P, KI, SEQ], bf16)
        qT = sb("qT", [P, 2, KD, SEQ], bf16)
        xs = [sb(f"x_row{i}", [P, TT, DIM], f32) for i in range(2)]
        ctx_sb = sb("ctx_sb", [P, TT, DIM], f32)
        ctxT = sb("ctxT", [P, KD, SEQ], f32)
        lnT = sb("lnT", [P, KD, SEQ], f32)
        z = lnT[:, :, :].rearrange("p (s a) n -> p s (a n)", s=2)
        probs = sb("probs", [P, TT, SEQ], f32)
        qrow = sb("qrow", [P, 2, DIM], bf16)
        stage = qrow[:, :, :].rearrange("p a n -> p (a n)").bitcast(f32).rearrange("p (s n) -> p s n", s=2)
        zmag = sb("zmag", [P, DIM], bf16)
        act_sb = sb("act_sb", [P, 2, 512], f32)
        hmag = sb("hmag", [P, 512], bf16)
        ident = sb("ident", [P, P], f32)
        ident_b = sb("ident_b", [P, P], bf16)
        sc = sb("sc", [P, 8], f32)
        fac = sb("fac", [P, 8], f32)
        stats = sb("stats", [P, TT, HALVES, 6], f32)
        mv = sb("mv", [P, TT, 2], f32)
        veps = sb("veps", [P, TT], f32)
        rstd = sb("rstd", [P, TT], f32)
        nhalf = sb("nhalf", [P, TT], f32)
        nm = sb("nm", [P, TT], f32)
        rs2 = sb("rs2", [P, 2, TT], f32)
        nm2 = sb("nm2", [P, 2, TT], f32)
        mx = sb("mx", [P, TT], f32)
        nmx = sb("nmx", [P, TT], f32)
        den = sb("den", [P, TT], f32)
        rden = sb("rden", [P, TT], f32)

        ps_gate = [ps("ps_gate0"), ps("ps_gate1")]
        ps_up = [ps("ps_up0"), ps("ps_up1")]
        ps_down = [ps("ps_down0"), ps("ps_down1")]
        ps_misc = [ps("ps_misc0"), ps("ps_misc1")]

        s_scal = sem("scalars_loaded")
        s_x = [[sem(f"x_loaded{i}_{t}") for t in range(TT)] for i in range(2)]
        s_ctx = sem("ctx_loaded")
        s_ctxt = sem("ctxT_loaded")
        s_wgu = [sem(f"gate_up_weights{p}") for p in range(PAIRS)]
        s_wd = [sem(f"down_weights{h}") for h in range(2)]
        s_store = [sem(f"out_stored{t}") for t in range(TT)]
        s_pad = sem("padding_zeroed")
        s_ident = sem("identity_zeroed")
        s_const = sem("constants_ready")
        s_tanh = sem("tanh_ready")
        s_fac = sem("factors_ready")
        s_var = sem("variance_ready")
        s_rstd = sem("rstd_ready")
        s_nm1 = sem("norm1_ready")
        s_staged = sem("ln_staged")
        s_lnx = sem("ln_transposed")
        s_lne = sem("lnT_written")
        s_score = sem("scores_done")
        s_max = sem("max_ready")
        s_exp = sem("exp_done")
        s_prob = sem("probs_ready")
        s_att = sem("attended")
        s_x1 = sem("x1_ready")
        s_nm2 = sem("norm2_ready")
        s_z = sem("z_ready")
        s_q = sem("q_ready")
        s_qx = sem("q_transposed")
        s_qe = sem("qT_written")
        s_gate = sem("gate_done")
        s_up = sem("up_done")
        s_silu = sem("silu_done")
        s_h = sem("hidden_made")
        s_hq = sem("hidden_quantised")
        s_down = sem("down_done")
        s_out = sem("out_ready")
        s_dve = sem("dve_chain")

        NG = TT * HALVES
        NJ = 2 * TT
        block = es.enter_context(nc.Block())

        @block.sync
        def _(sp):
            sp.dma_start(sc[:, :], scalars.to_broadcast([P, 8])).then_inc(s_scal, 16)

            def load_x(a, t, odd):
                sp.dma_start(xs[odd][:, t, :], x[bass.ds(a, 1), t * P:(t + 1) * P, :].rearrange("o p n -> p (o n)"))\
                    .then_inc(s_x[odd][t], 16)

            def load_ctxt(a):
                sp.dma_start(ctxT[:, :, :], ctx_t[bass.ds(a, 1), :, :, :].rearrange("o p k n -> p (o k) n"))\
                    .then_inc(s_ctxt, 16)

            def load_ctx(a):
                sp.dma_start(ctx_sb[:, :, :], ctx[bass.ds(a, 1), :, :].rearrange("o (t p) n -> p (o t) n", p=P))\
                    .then_inc(s_ctx, 16)

            def store(b, t, odd):
                sp.wait_ge(s_out, NG * b + HALVES * (t + 1))
                sp.dma_start(out[bass.ds(b, 1), t * P:(t + 1) * P, :].rearrange("o p n -> p (o n)"), xs[odd][:, t, :])\
                    .then_inc(s_store[t], 16)

            def row(b, odd, following):
                if following:
                    sp.wait_ge(s_score, b + 2)
                    load_ctxt(b + 2)
                    sp.wait_ge(s_att, NG * b + 2 * NG)
                    load_ctx(b + 2)
                for t in range(TT):
                    store(b, t, odd)
                if following:
                    for t in range(TT):
                        sp.wait_ge(s_store[t], 16 * b + 16)
                        load_x(b + 2, t, odd)

            for t in range(TT):
                load_x(0, t, 0)
            load_ctxt(0)
            load_ctx(0)
            for t in range(TT):
                load_x(1, t, 1)
            sp.wait_ge(s_score, 1)
            load_ctxt(1)
            sp.wait_ge(s_att, NG)
            load_ctx(1)
            with sp.Fori(0, BATCH - 3, 2) as b:
                row(b, 0, True)
                row(b + 1, 1, True)
            row(BATCH - 2, 0, False)
            row(BATCH - 1, 1, False)
            for t in range(TT):
                sp.wait_ge(s_store[t], 16 * BATCH)

        @block.gpsimd
        def _(pool):
            pool.memset(w_gate[:, FULL, :, TAIL:256], 0.0).then_inc(s_pad, 1)
            pool.memset(w_up[:, FULL, :, TAIL:256], 0.0).then_inc(s_pad, 1)
            pool.wait_ge(s_pad, 2)
            pool.memset(w_down[DTAIL:P, KI - 1, :], 0.0).then_inc(s_pad, 1)
            pool.wait_ge(s_pad, 3)
            pool.memset(nhalf[:, :], -0.5).then_inc(s_const, 1)
            pool.memset(ident[:, :], 0.0).then_inc(s_ident, 1)
            pool.memset(ident_b[:, :], 0.0).then_inc(s_ident, 1)
            pool.wait_ge(s_ident, 2)
            for m in (ident, ident_b):
                pool.affine_select(out=m[:, :], in_=m[:, :], compare_op=ALU.not_equal, fill=1.0,
                                   base=0, pattern=[[-1, P]], channel_multiplier=1).then_inc(s_const, 1)
            for p in range(FULL):
                pool.dma_start(w_gate[:, p, :, :], gate_main[:, p, :, :]).then_inc(s_wgu[p], 16)
                pool.dma_start(w_up[:, p, :, :], up_main[:, p, :, :]).then_inc(s_wgu[p], 16)
            pool.dma_start(w_gate[:, FULL, :, 0:TAIL], gate_tail).then_inc(s_wgu[FULL], 16)
            pool.dma_start(w_up[:, FULL, :, 0:TAIL], up_tail).then_inc(s_wgu[FULL], 16)
            half = KI // 2
            pool.dma_start(w_down[:, 0:half, :], down_main[:, 0:half, :]).then_inc(s_wd[0], 16)
            pool.dma_start(w_down[:, half:KI - 1, :], down_main[:, half:KI - 1, :]).then_inc(s_wd[1], 16)
            pool.dma_start(w_down[0:DTAIL, KI - 1, :], down_tail).then_inc(s_wd[1], 16)

            def inverse_root(n):
                pool.wait_ge(s_var, n + 1)
                pool.tensor_tensor(rstd[:, :], veps[:, :], nhalf[:, :], ALU.pow).then_inc(s_rstd, 1)

            pool.wait_ge(s_const, 1)
            inverse_root(0)
            inverse_root(1)
            with pool.Fori(1, BATCH) as a:
                inverse_root(2 * a)
                inverse_root(2 * a + 1)

        @block.scalar
        def _(act):
            act.wait_ge(s_scal, 16)
            act.activation(fac[:, 0:2], sc[:, 0:2], ACT.Tanh).then_inc(s_tanh, 1)

            def ln_stage(a, i, odd):
                t, h = divmod(i, HALVES)
                if i == 0:
                    act.wait_ge(s_nm1, a + 1)
                if i >= 2:
                    act.wait_ge(s_lnx, NG * a + i - 1)
                act.activation(stage[:, i % 2, :], xs[odd][:, t, h * 512:(h + 1) * 512], ACT.Identity,
                               bias=nm[:, t:t + 1], scale=rstd[:, t:t + 1]).then_inc(s_staged, 1)

            def ln_evac(a, i):
                t, h = divmod(i, HALVES)
                act.wait_ge(s_lnx, NG * a + i + 1)
                act.activation(lnT[:, 4 * h:4 * h + 4, t * P:(t + 1) * P],
                               ps_misc[i % 2][:, :].rearrange("p (k n) -> p k n", n=P), ACT.Copy)\
                    .then_inc(s_lne, 1)

            def ln1(a, odd):
                ln_stage(a, 0, odd)
                ln_stage(a, 1, odd)
                ln_evac(a, 0)
                ln_stage(a, 2, odd)
                ln_evac(a, 1)
                ln_stage(a, 3, odd)
                ln_evac(a, 2)
                ln_evac(a, 3)

            def exps(a):
                act.wait_ge(s_max, a + 1)
                for t in range(TT):
                    e = act.activation(probs[:, t, :], ps_misc[0][:, t * SEQ:(t + 1) * SEQ], ACT.Exp,
                                       bias=nmx[:, t:t + 1], scale=SCORE_SCALE, accum_out=den[:, t:t + 1])
                e.then_inc(s_exp, 1)

            def make_z(a, j, odd):
                t, w = divmod(j, 2)
                if j == 0:
                    act.wait_ge(s_nm2, a + 1)
                if j >= 2:
                    act.wait_ge(s_q, NJ * a + j - 1)
                act.activation(z[:, j % 2, :], xs[odd][:, t, :], ACT.Identity,
                               bias=nm2[:, w, t:t + 1], scale=rs2[:, w, t:t + 1]).then_inc(s_z, 1)

            def q_evac(a, j):
                t, w = divmod(j, 2)
                act.wait_ge(s_qx, NJ * a + j + 1)
                act.activation(qT[:, w, :, t * P:(t + 1) * P],
                               ps_misc[(j + 1) % 2][:, :].bitcast(bf16).rearrange("p (k n) -> p k n", n=P), ACT.Copy)\
                    .then_inc(s_qe, 1)

            def silu(b, p):
                act.wait_ge(s_gate, PAIRS * b + p + 1)
                if p >= 2:
                    act.wait_ge(s_hq, PAIRS * b + p - 1)
                else:
                    if not (isinstance(b, int) and b == 0):
                        act.wait_ge(s_hq, PAIRS * b + p - 1)
                act.activation(act_sb[:, p % 2, :], ps_gate[p % 2][:, :], ACT.Silu,
                               scale=fac[:, 2:3]).then_inc(s_silu, 1)

            ln1(0, 0)
            exps(0)
            for j in range(NJ):
                make_z(0, j, 0)
                if j >= 1:
                    q_evac(0, j - 1)
            q_evac(0, NJ - 1)
            act.wait_ge(s_fac, 1)

            def row(b, odd, following):
                a = b + 1
                for p in range(PAIRS):
                    if following and p == 3:
                        ln1(a, 1 - odd)
                    if following and p == 5:
                        exps(a)
                    if following and p == 9:
                        make_z(a, 0, 1 - odd)
                        make_z(a, 1, 1 - odd)
                    silu(b, p)
                if following:
                    q_evac(a, 0)
                    make_z(a, 2, 1 - odd)
                    q_evac(a, 1)
                    make_z(a, 3, 1 - odd)
                    q_evac(a, 2)
                    q_evac(a, 3)

            row(0, 0, True)
            with act.Fori(1, BATCH - 2, 2) as b:
                row(b, 1, True)
                row(b + 1, 0, True)
            row(BATCH - 1, 1, False)

        @block.tensor
        def _(pe):
            pe.wait_ge(s_const, 3)

            def ln_transposes(a, i):
                pe.wait_ge(s_staged, NG * a + i + 1)
                if i >= 2:
                    pe.wait_ge(s_lne, NG * a + i - 1)
                else:
                    if not (isinstance(a, int) and a == 0):
                        pe.wait_ge(s_qe, NJ * a)
                for k in range(4):
                    m = pe.transpose(ps_misc[i % 2][:, k * P:(k + 1) * P], stage[:, i % 2, k * P:(k + 1) * P],
                                     ident[:, :])
                m.then_inc(s_lnx, 1)

            def scores(a):
                pe.wait_ge(s_lne, NG * a + NG)
                pe.wait_ge(s_ctxt, 16 * a + 16)
                for t in range(TT):
                    for k in range(KD):
                        m = pe.matmul(ps_misc[0][:, t * SEQ:(t + 1) * SEQ], lnT[:, k, t * P:(t + 1) * P],
                                      ctxT[:, k, :], start=(k == 0), stop=(k == KD - 1))
                m.then_inc(s_score, 1)

            def attend(a, g):
                c, h = divmod(g, HALVES)
                if g == 0:
                    pe.wait_ge(s_prob, a + 1)
                    pe.wait_ge(s_ctx, 16 * a + 16)
                if g >= 2:
                    pe.wait_ge(s_x1, NG * a + g - 1)
                for t in range(TT):
                    m = pe.matmul(ps_misc[(g + 1) % 2][:, :], probs[:, t, c * P:(c + 1) * P],
                                  ctx_sb[:, t, h * 512:(h + 1) * 512], start=(t == 0), stop=(t == TT - 1))
                m.then_inc(s_att, 1)

            def q_transposes(a, j):
                pe.wait_ge(s_q, NJ * a + j + 1)
                if j >= 2:
                    pe.wait_ge(s_qe, NJ * a + j - 1)
                else:
                    pe.wait_ge(s_x1, NG * a + NG - 1 + j)
                for k in range(KD):
                    m = pe.transpose(ps_misc[(j + 1) % 2][:, :].bitcast(bf16)[:, k * P:(k + 1) * P],
                                     qrow[:, j % 2, k * P:(k + 1) * P], ident_b[:, :])
                m.then_inc(s_qx, 1)

            def gate_up(b, p):
                if p == 0:
                    pe.wait_ge(s_qe, NJ * b + NJ)
                pe.wait_ge(s_wgu[p], 32)
                if p >= 2:
                    pe.wait_ge(s_h, PAIRS * b + p - 1)
                else:
                    if not (isinstance(b, int) and b == 0):
                        pe.wait_ge(s_h, PAIRS * b + p - 1)
                for w, wt, bank, done in ((0, w_gate, ps_gate, s_gate), (1, w_up, ps_up, s_up)):
                    for i in range(2):
                        for k in range(KD):
                            m = pe.matmul(bank[p % 2][:, i * SEQ:(i + 1) * SEQ], wt[:, p, k, i * P:(i + 1) * P],
                                          qT[:, w, k, :], start=(k == 0), stop=(k == KD - 1))
                    m.then_inc(done, 1)

            def down(b, g):
                t, h = divmod(g, HALVES)
                if g >= 2:
                    pe.wait_ge(s_out, NG * b + g - 1)
                else:
                    if not (isinstance(b, int) and b == 0):
                        pe.wait_ge(s_out, NG * b + g - 1)
                for k in range(KI):
                    if g == 0 and k % 2 == 0:
                        pe.wait_ge(s_hq, PAIRS * b + k // 2 + 1)
                    if k == 0:
                        pe.wait_ge(s_wd[0], 16)
                    if k == KI // 2:
                        pe.wait_ge(s_wd[1], 32)
                    m = pe.matmul(ps_down[g % 2][:, :], hq[:, k, t * P:(t + 1) * P],
                                  w_down[:, k, h * 512:(h + 1) * 512], start=(k == 0), stop=(k == KI - 1))
                m.then_inc(s_down, 1)

            for i in range(NG):
                ln_transposes(0, i)
            scores(0)
            for g in range(NG):
                attend(0, g)
            for j in range(NJ):
                q_transposes(0, j)
            pe.wait_ge(s_pad, 3)

            def row(b, odd, following):
                a = b + 1
                for p in range(PAIRS):
                    gate_up(b, p)
                    if following:
                        if p == 2:
                            for i in range(NG):
                                ln_transposes(a, i)
                        if p == 3:
                            scores(a)
                        if p == 5:
                            attend(a, 0)
                            attend(a, 1)
                        if p == 6:
                            attend(a, 2)
                            attend(a, 3)
                for g in range(NG):
                    down(b, g)
                    if following and g >= 1:
                        q_transposes(a, g - 1)
                if following:
                    q_transposes(a, NJ - 1)

            row(0, 0, True)
            with pe.Fori(1, BATCH - 2, 2) as b:
                row(b, 1, True)
                row(b + 1, 0, True)
            row(BATCH - 1, 1, False)

        @block.vector
        def _(dve):
            link = [0]

            def then(ins):
                link[0] += 1
                ins.then_inc(s_dve, 1)
                dve.wait_ge(s_dve, link[0])

            def fence():
                dve.sem_clear(s_dve)
                link[0] = 0

            dve.wait_ge(s_scal, 16)
            then(dve.reciprocal(fac[:, 5:8], sc[:, 5:8]))
            dve.tensor_tensor(fac[:, 2:3], sc[:, 2:3], sc[:, 5:6], ALU.mult)
            then(dve.scalar_tensor_tensor(out=fac[:, 3:4], in0=sc[:, 3:4], scalar=sc[:, 6:7], in1=fac[:, 7:8],
                                          op0=ALU.mult, op1=ALU.mult))
            dve.wait_ge(s_tanh, 1)
            dve.scalar_tensor_tensor(out=fac[:, 4:5], in0=sc[:, 4:5], scalar=sc[:, 7:8], in1=fac[:, 1:2],
                                     op0=ALU.mult, op1=ALU.mult).then_inc(s_fac, 1)

            def layer_stats(a, second, odd):
                for t in range(TT):
                    if not second:
                        dve.wait_ge(s_x[odd][t], 8 * a + 16 - 8 * odd)
                    for h in range(HALVES):
                        last = dve.bn_stats(stats[:, t, h, :], xs[odd][:, t, h * 512:(h + 1) * 512])
                then(last)
                for t in range(TT):
                    last = dve.bn_aggr(mv[:, t, :], stats[:, t, :, :].rearrange("p h s -> p (h s)"))
                then(last)
                dve.tensor_scalar(veps[:, :], mv[:, :, 1], EPS, None, ALU.add).then_inc(s_var, 1)

            def norm1(a):
                dve.wait_ge(s_rstd, 2 * a + 1)
                dve.scalar_tensor_tensor(out=nm[:, :], in0=mv[:, :, 0], scalar=-1.0, in1=rstd[:, :],
                                         op0=ALU.mult, op1=ALU.mult).then_inc(s_nm1, 1)

            def norm2(a):
                dve.wait_ge(s_rstd, 2 * a + 2)
                for w in range(2):
                    last = dve.tensor_scalar(rs2[:, w, :], rstd[:, :], fac[:, 5 + w:6 + w], None, ALU.mult)
                then(last)
                for w in range(2):
                    last = dve.scalar_tensor_tensor(out=nm2[:, w, :], in0=mv[:, :, 0], scalar=-1.0,
                                                    in1=rs2[:, w, :], op0=ALU.mult, op1=ALU.mult)
                last.then_inc(s_nm2, 1)

            def maxima(a):
                dve.wait_ge(s_score, a + 1)
                then(dve.reduce_max(mx[:, :], ps_misc[0][:, :].rearrange("p (t c) -> p t c", t=TT), AX.X))
                dve.tensor_scalar(nmx[:, :], mx[:, :], -SCORE_SCALE, None, ALU.mult).then_inc(s_max, 1)

            def normalise(a):
                dve.wait_ge(s_exp, a + 1)
                then(dve.reciprocal(rden[:, :], den[:, :]))
                for t in range(TT):
                    last = dve.tensor_scalar(probs[:, t, :], probs[:, t, :], rden[:, t:t + 1], None, ALU.mult)
                last.then_inc(s_prob, 1)

            def residual1(a, g, odd):
                c, h = divmod(g, HALVES)
                dve.wait_ge(s_att, NG * a + g + 1)
                at = xs[odd][:, c, h * 512:(h + 1) * 512]
                return dve.scalar_tensor_tensor(out=at, in0=ps_misc[(g + 1) % 2][:, :], scalar=fac[:, 0:1], in1=at,
                                                op0=ALU.mult, op1=ALU.add).then_inc(s_x1, 1)

            def round_e4m3(v, mag, q):
                high = v.bitcast(u16).rearrange("p (n two) -> p n two", two=2)[:, :, 1]
                then(dve.tensor_scalar(mag.bitcast(u16), high, 0x7F80, 0x0040, ALU.bitwise_and, ALU.bitwise_or))
                then(dve.tensor_scalar(mag, mag, 1.5 * MIN_NORMAL, 1.5 * 2.0 ** 8, ALU.max, ALU.min))
                then(dve.scalar_tensor_tensor(out=v, in0=mag, scalar=ROUND, in1=v, op0=ALU.mult, op1=ALU.add))
                then(dve.scalar_tensor_tensor(out=q, in0=mag, scalar=-ROUND, in1=v, op0=ALU.mult, op1=ALU.add))
                return dve.tensor_scalar(q, q, FP8_MAX, -FP8_MAX, ALU.min, ALU.max)

            def quantise_row(a, j):
                dve.wait_ge(s_z, NJ * a + j + 1)
                if j >= 2:
                    dve.wait_ge(s_qx, NJ * a + j - 1)
                round_e4m3(z[:, j % 2, :], zmag[:, :], qrow[:, j % 2, :]).then_inc(s_q, 1)

            def hidden(b, p):
                dve.wait_ge(s_silu, PAIRS * b + p + 1)
                dve.wait_ge(s_up, PAIRS * b + p + 1)
                if p == 0 and not (isinstance(b, int) and b == 0):
                    dve.wait_ge(s_down, NG * b)
                v = act_sb[:, p % 2, :]
                ins = dve.scalar_tensor_tensor(out=v, in0=ps_up[p % 2][:, :], scalar=fac[:, 3:4], in1=v,
                                               op0=ALU.mult, op1=ALU.mult)
                ins.then_inc(s_h, 1)
                dve.wait_ge(s_h, PAIRS * b + p + 1)
                round_e4m3(v, hmag[:, :], hq[:, 2 * p:2 * p + 2, :].rearrange("p a n -> p (a n)")).then_inc(s_hq, 1)

            def residual2(b, g, odd):
                t, h = divmod(g, HALVES)
                dve.wait_ge(s_down, NG * b + g + 1)
                at = xs[odd][:, t, h * 512:(h + 1) * 512]
                dve.scalar_tensor_tensor(out=at, in0=ps_down[g % 2][:, :], scalar=fac[:, 4:5], in1=at,
                                         op0=ALU.mult, op1=ALU.add).then_inc(s_out, 1)

            def attended(a, odd):
                for g in range(NG):
                    residual1(a, g, odd)
                dve.wait_ge(s_x1, NG * a + NG)
                layer_stats(a, True, odd)

            layer_stats(0, False, 0)
            norm1(0)
            maxima(0)
            normalise(0)
            dve.wait_ge(s_fac, 1)
            attended(0, 0)
            norm2(0)
            for j in range(NJ):
                quantise_row(0, j)

            def row(b, odd, following):
                fence()
                a = b + 1
                for p in range(PAIRS):
                    if following:
                        if p == 1:
                            layer_stats(a, False, 1 - odd)
                        if p == 2:
                            norm1(a)
                        if p == 4:
                            maxima(a)
                        if p == 5:
                            normalise(a)
                        if p == 7:
                            attended(a, 1 - odd)
                        if p == 8:
                            norm2(a)
                        if p == 10:
                            quantise_row(a, 0)
                    hidden(b, p)
                if following:
                    quantise_row(a, 1)
                residual2(b, 0, odd)
                residual2(b, 1, odd)
                if following:
                    quantise_row(a, 2)
                residual2(b, 2, odd)
                if following:
                    quantise_row(a, 3)
                residual2(b, 3, odd)

            row(0, 0, True)
            with dve.Fori(1, BATCH - 2, 2) as b:
                row(b, 1, True)
                row(b + 1, 0, True)
            row(BATCH - 1, 1, False)


def kernel(x, ctx_4096, g_xattn, g_ffn, L0_ffn_gate_w, L0_ffn_up_w, L0_ffn_down_w, L0_ffn_gate_w_scale,
           L0_ffn_up_w_scale, L0_ffn_down_w_scale, L0_ffn_gate_in_scale, L0_ffn_up_in_scale, L0_ffn_down_in_scale):
    import numpy as np
    import concourse.bacc as bacc
    from concourse.bass_utils import run_bass_kernel_spmd

    def up_pairs(w):
        w = np.asarray(w)
        main = w[:FULL * 256].reshape(FULL, 256, KD, P).transpose(3, 0, 2, 1)
        tail = w[FULL * 256:].reshape(TAIL, KD, P).transpose(2, 1, 0)
        return np.ascontiguousarray(main), np.ascontiguousarray(tail)

    gate_main, gate_tail = up_pairs(L0_ffn_gate_w)
    up_main, up_tail = up_pairs(L0_ffn_up_w)
    down = np.asarray(L0_ffn_down_w)
    down_main = np.ascontiguousarray(down[:, :(KI - 1) * P].reshape(DIM, KI - 1, P).transpose(2, 1, 0))
    down_tail = np.ascontiguousarray(down[:, (KI - 1) * P:].transpose(1, 0))
    ctx = np.ascontiguousarray(np.asarray(ctx_4096))
    ctx_t = np.ascontiguousarray(ctx.reshape(BATCH, SEQ, KD, P).transpose(0, 3, 2, 1))
    scalars = np.concatenate([np.asarray(s).reshape(1, 1) for s in (
        g_xattn, g_ffn, L0_ffn_gate_w_scale, L0_ffn_up_w_scale, L0_ffn_down_w_scale,
        L0_ffn_gate_in_scale, L0_ffn_up_in_scale, L0_ffn_down_in_scale)], axis=1)

    nc = bacc.Bacc("TRN2", target_bir_lowering=False, num_devices=1)
    arrays, args = {}, []
    for name, a in (("x", np.ascontiguousarray(np.asarray(x))), ("ctx", ctx), ("ctx_t", ctx_t), ("scalars", scalars),
                    ("gate_main", gate_main), ("gate_tail", gate_tail), ("up_main", up_main),
                    ("up_tail", up_tail), ("down_main", down_main), ("down_tail", down_tail)):
        arrays[name] = a
        args.append(nc.dram_tensor(name, a.shape, mybir.dt.from_np(a.dtype), kind="ExternalInput").ap())
    args.append(nc.dram_tensor("out", (BATCH, SEQ, DIM), mybir.dt.float32, kind="ExternalOutput").ap())
    gated_xattn_ffn(nc, *args)
    r = run_bass_kernel_spmd(nc, [arrays], core_ids=[0])
    return r.results[0]["out"]
```

```python
from contextlib import ExitStack

import concourse.bass as bass
from concourse import mybir

P = 128
BATCH, SEQ, DIM, INNER = 8, 256, 1024, 2752
TT = SEQ // P
KD = DIM // P
HALVES = DIM // 512
PAIRS = -(-INNER // 256)
KI = 2 * PAIRS
TAIL = INNER - (PAIRS - 1) * 256
DTAIL = INNER - (KI - 1) * P
FULL = PAIRS - 1
EPS = 1e-5
FP8_MAX = 448.0
MIN_NORMAL = 2.0 ** -6
ROUND = 2.0 ** 20
SCORE_SCALE = float(SEQ) ** -0.5


def gated_xattn_ffn(nc, x, ctx, ctx_t, scalars, gate_main, gate_tail, up_main, up_tail,
                    down_main, down_tail, out):
    f32, bf16, u16 = mybir.dt.float32, mybir.dt.bfloat16, mybir.dt.uint16
    ALU, ACT, AX = mybir.AluOpType, mybir.ActivationFunctionType, mybir.AxisListType

    es = ExitStack()
    with es:
        def sb(name, shape, dt):
            return es.enter_context(nc.sbuf_tensor(name, shape, dt))

        def ps(name):
            return es.enter_context(nc.psum_tensor(name, [P, 512], f32))

        def sem(name):
            return es.enter_context(nc.semaphore(name))

        w_gate = sb("w_gate", [P, PAIRS, KD, 256], bf16)
        w_up = sb("w_up", [P, PAIRS, KD, 256], bf16)
        w_down = sb("w_down", [P, KI, DIM], bf16)
        hq = sb("hq", [P, KI, SEQ], bf16)
        qT = sb("qT", [P, 2, KD, SEQ], bf16)
        xs = [sb(f"x_row{i}", [P, TT, DIM], f32) for i in range(2)]
        ctx_sb = sb("ctx_sb", [P, TT, DIM], f32)
        ctxT = sb("ctxT", [P, KD, SEQ], f32)
        lnT = sb("lnT", [P, KD, SEQ], f32)
        probs = lnT[:, 0:TT, :]
        z = lnT[:, :, :].rearrange("p (s a) n -> p s (a n)", s=2)
        qrow = sb("qrow", [P, 2, DIM], bf16)
        stage = qrow[:, :, :].rearrange("p a n -> p (a n)").bitcast(f32).rearrange("p (s n) -> p s n", s=2)
        zmag = sb("zmag", [P, 2, DIM], bf16)
        act_sb = sb("act_sb", [P, 2, 512], f32)
        hmag = sb("hmag", [P, 2, 512], bf16)
        ident = sb("ident", [P, P], f32)
        ident_b = sb("ident_b", [P, P], bf16)
        sc = sb("sc", [P, 8], f32)
        fac = sb("fac", [P, 8], f32)
        stats = sb("stats", [P, TT, HALVES, 6], f32)
        mv = sb("mv", [P, TT, 2], f32)
        veps = sb("veps", [P, TT], f32)
        rstd = sb("rstd", [P, TT], f32)
        nhalf = sb("nhalf", [P, TT], f32)
        nm = sb("nm", [P, TT], f32)
        rs2 = sb("rs2", [P, 2, TT], f32)
        nm2 = sb("nm2", [P, 2, TT], f32)
        rs2r = sb("rs2r", [P, 2, TT], f32)
        nm2r = sb("nm2r", [P, 2, TT], f32)
        mx = sb("mx", [P, TT], f32)
        nmx = sb("nmx", [P, TT], f32)
        den = sb("den", [P, TT], f32)
        rden = sb("rden", [P, TT], f32)

        ps_gate = [ps("ps_gate0"), ps("ps_gate1")]
        ps_up = [ps("ps_up0"), ps("ps_up1")]
        ps_down = [ps("ps_down0"), ps("ps_down1")]
        ps_misc = [ps("ps_misc0"), ps("ps_misc1")]

        s_scal = sem("scalars_loaded")
        s_x = [[sem(f"x_loaded{i}_{t}") for t in range(TT)] for i in range(2)]
        s_ctx = sem("ctx_loaded")
        s_ctxt = sem("ctxT_loaded")
        s_wgu = [sem(f"gate_up_weights{p}") for p in range(PAIRS)]
        s_wd = [sem(f"down_weights{h}") for h in range(2)]
        s_store = [sem(f"out_stored{t}") for t in range(TT)]
        s_pad = sem("padding_zeroed")
        s_ident = sem("identity_zeroed")
        s_const = sem("constants_ready")
        s_tanh = sem("tanh_ready")
        s_fac = sem("factors_ready")
        s_var = sem("variance_ready")
        s_rstd = sem("rstd_ready")
        s_nm1 = sem("norm1_ready")
        s_staged = sem("ln_staged")
        s_lnx = sem("ln_transposed")
        s_lne = sem("lnT_written")
        s_score = sem("scores_done")
        s_max = sem("max_ready")
        s_exp = sem("exp_done")
        s_prob = sem("probs_ready")
        s_att = sem("attended")
        s_x1 = sem("x1_ready")
        s_nm2 = sem("norm2_ready")
        s_zmag = sem("scaled_z_ready")
        s_z = sem("z_ready")
        s_q = sem("q_ready")
        s_qx = sem("q_transposed")
        s_qe = sem("qT_written")
        s_gate = sem("gate_done")
        s_up = sem("up_done")
        s_silu = sem("silu_done")
        s_h = sem("hidden_made")
        s_hq = sem("hidden_quantised")
        s_down = sem("down_done")
        s_out = sem("out_ready")
        s_dve = sem("dve_chain")

        NG = TT * HALVES
        NJ = 2 * TT

        def first(b):
            return isinstance(b, int) and b == 0

        block = es.enter_context(nc.Block())

        @block.sync
        def _(sp):
            sp.dma_start(sc[:, :], scalars.to_broadcast([P, 8])).then_inc(s_scal, 16)

            def load_x(a, t, odd):
                sp.dma_start(xs[odd][:, t, :], x[bass.ds(a, 1), t * P:(t + 1) * P, :].rearrange("o p n -> p (o n)"))\
                    .then_inc(s_x[odd][t], 16)

            def load_ctxt(a):
                sp.dma_start(ctxT[:, :, :], ctx_t[bass.ds(a, 1), :, :, :].rearrange("o p k n -> p (o k) n"))\
                    .then_inc(s_ctxt, 16)

            def load_ctx(a):
                sp.dma_start(ctx_sb[:, :, :], ctx[bass.ds(a, 1), :, :].rearrange("o (t p) n -> p (o t) n", p=P))\
                    .then_inc(s_ctx, 16)

            def store(b, t, odd):
                sp.wait_ge(s_out, NG * b + HALVES * (t + 1))
                sp.dma_start(out[bass.ds(b, 1), t * P:(t + 1) * P, :].rearrange("o p n -> p (o n)"), xs[odd][:, t, :])\
                    .then_inc(s_store[t], 16)

            def row(b, odd, following):
                if following:
                    sp.wait_ge(s_score, b + 2)
                    load_ctxt(b + 2)
                    sp.wait_ge(s_att, NG * b + 2 * NG)
                    load_ctx(b + 2)
                for t in range(TT):
                    store(b, t, odd)
                    if following:
                        sp.wait_ge(s_store[t], 16 * b + 16)
                        load_x(b + 2, t, odd)

            for t in range(TT):
                load_x(0, t, 0)
            load_ctxt(0)
            load_ctx(0)
            for t in range(TT):
                load_x(1, t, 1)
            sp.wait_ge(s_score, 1)
            load_ctxt(1)
            sp.wait_ge(s_att, NG)
            load_ctx(1)
            with sp.Fori(0, BATCH - 3, 2) as b:
                row(b, 0, True)
                row(b + 1, 1, True)
            row(BATCH - 2, 0, False)
            row(BATCH - 1, 1, False)
            for t in range(TT):
                sp.wait_ge(s_store[t], 16 * BATCH)

        @block.gpsimd
        def _(pool):
            pool.memset(w_gate[:, FULL, :, TAIL:256], 0.0).then_inc(s_pad, 1)
            pool.memset(w_up[:, FULL, :, TAIL:256], 0.0).then_inc(s_pad, 1)
            pool.wait_ge(s_pad, 2)
            pool.memset(w_down[DTAIL:P, KI - 1, :], 0.0).then_inc(s_pad, 1)
            pool.wait_ge(s_pad, 3)
            pool.memset(nhalf[:, :], -0.5).then_inc(s_const, 1)
            pool.memset(ident[:, :], 0.0).then_inc(s_ident, 1)
            pool.memset(ident_b[:, :], 0.0).then_inc(s_ident, 1)
            pool.wait_ge(s_const, 1)
            pool.wait_ge(s_ident, 2)
            for m in (ident, ident_b):
                pool.affine_select(out=m[:, :], in_=m[:, :], compare_op=ALU.not_equal, fill=1.0,
                                   base=0, pattern=[[-1, P]], channel_multiplier=1).then_inc(s_const, 1)

            def inverse_root(n, t0, t1):
                pool.wait_ge(s_var, n + 1)
                pool.tensor_tensor(rstd[:, t0:t1], veps[:, t0:t1], nhalf[:, t0:t1], ALU.pow).then_inc(s_rstd, 1)

            def roots(a):
                for t in range(TT):
                    inverse_root(3 * a + t, t, t + 1)
                inverse_root(3 * a + TT, 0, TT)

            def load_pair(p):
                pool.dma_start(w_gate[:, p, :, :], gate_main[:, p, :, :]).then_inc(s_wgu[p], 16)
                pool.dma_start(w_up[:, p, :, :], up_main[:, p, :, :]).then_inc(s_wgu[p], 16)

            load_pair(0)
            load_pair(1)
            for t in range(TT):
                inverse_root(t, t, t + 1)
            for p in range(2, FULL):
                load_pair(p)
            pool.dma_start(w_gate[:, FULL, :, 0:TAIL], gate_tail).then_inc(s_wgu[FULL], 16)
            pool.dma_start(w_up[:, FULL, :, 0:TAIL], up_tail).then_inc(s_wgu[FULL], 16)
            inverse_root(TT, 0, TT)
            half = KI // 2
            pool.dma_start(w_down[:, 0:half, :], down_main[:, 0:half, :]).then_inc(s_wd[0], 16)
            pool.dma_start(w_down[:, half:KI - 1, :], down_main[:, half:KI - 1, :]).then_inc(s_wd[1], 16)
            pool.dma_start(w_down[0:DTAIL, KI - 1, :], down_tail).then_inc(s_wd[1], 16)
            with pool.Fori(1, BATCH) as a:
                roots(a)

        @block.scalar
        def _(act):
            act.wait_ge(s_scal, 16)
            act.activation(fac[:, 0:2], sc[:, 0:2], ACT.Tanh).then_inc(s_tanh, 1)

            def ln_stage(a, i, odd):
                t, h = divmod(i, HALVES)
                if h == 0:
                    act.wait_ge(s_nm1, TT * a + t + 1)
                if i >= 2:
                    act.wait_ge(s_lnx, NG * a + i - 1)
                act.activation(stage[:, i % 2, :], xs[odd][:, t, h * 512:(h + 1) * 512], ACT.Identity,
                               bias=nm[:, t:t + 1], scale=rstd[:, t:t + 1]).then_inc(s_staged, 1)

            def ln_evac(a, i):
                t, h = divmod(i, HALVES)
                act.wait_ge(s_lnx, NG * a + i + 1)
                act.activation(lnT[:, 4 * h:4 * h + 4, t * P:(t + 1) * P],
                               ps_misc[i % 2][:, :].rearrange("p (k n) -> p k n", n=P), ACT.Copy)\
                    .then_inc(s_lne, 1)

            def exps(a):
                act.wait_ge(s_max, a + 1)
                for t in range(TT):
                    e = act.activation(probs[:, t, :], ps_misc[0][:, t * SEQ:(t + 1) * SEQ], ACT.Exp,
                                       bias=nmx[:, t:t + 1], scale=SCORE_SCALE, accum_out=den[:, t:t + 1])
                e.then_inc(s_exp, 1)

            def make_z(a, j, odd):
                w, t = divmod(j, TT)
                if j == 0:
                    act.wait_ge(s_nm2, a + 1)
                if j >= 2:
                    act.wait_ge(s_q, NJ * a + j - 1)
                act.activation(zmag[:, j % 2, :], xs[odd][:, t, :], ACT.Identity,
                               bias=nm2r[:, w, t:t + 1], scale=rs2r[:, w, t:t + 1]).then_inc(s_zmag, 1)
                act.activation(z[:, j % 2, :], xs[odd][:, t, :], ACT.Identity,
                               bias=nm2[:, w, t:t + 1], scale=rs2[:, w, t:t + 1]).then_inc(s_z, 1)

            def q_evac(a, j):
                w, t = divmod(j, TT)
                act.wait_ge(s_qx, NJ * a + j + 1)
                act.activation(qT[:, w, :, t * P:(t + 1) * P],
                               ps_misc[(j + 1) % 2][:, :].bitcast(bf16).rearrange("p (k n) -> p k n", n=P), ACT.Copy)\
                    .then_inc(s_qe, 1)

            def silu(b, p):
                act.wait_ge(s_gate, PAIRS * b + p + 1)
                if p >= 2 or not first(b):
                    act.wait_ge(s_hq, PAIRS * b + p - 1)
                act.activation(act_sb[:, p % 2, :], ps_gate[p % 2][:, :], ACT.Silu,
                               scale=fac[:, 2:3]).then_inc(s_silu, 1)

            ln_stage(0, 0, 0)
            ln_stage(0, 1, 0)
            ln_evac(0, 0)
            ln_stage(0, 2, 0)
            ln_evac(0, 1)
            ln_stage(0, 3, 0)
            ln_evac(0, 2)
            ln_evac(0, 3)
            exps(0)
            make_z(0, 0, 0)
            make_z(0, 1, 0)
            make_z(0, 2, 0)
            q_evac(0, 0)
            make_z(0, 3, 0)
            for j in range(1, NJ):
                q_evac(0, j)
            act.wait_ge(s_fac, 1)

            def row(b, odd, following):
                a = b + 1
                for p in range(PAIRS):
                    if following:
                        if p == 1:
                            ln_stage(a, 0, 1 - odd)
                            ln_stage(a, 1, 1 - odd)
                        if p == 2:
                            ln_evac(a, 0)
                            ln_evac(a, 1)
                        if p == 3:
                            ln_stage(a, 2, 1 - odd)
                            ln_stage(a, 3, 1 - odd)
                        if p == 4:
                            ln_evac(a, 2)
                            ln_evac(a, 3)
                        if p == 5:
                            exps(a)
                        if p == 8:
                            make_z(a, 0, 1 - odd)
                        if p == 9:
                            make_z(a, 1, 1 - odd)
                    silu(b, p)
                if following:
                    make_z(a, 2, 1 - odd)
                    q_evac(a, 0)
                    make_z(a, 3, 1 - odd)
                    q_evac(a, 1)
                    q_evac(a, 2)
                    q_evac(a, 3)

            row(0, 0, True)
            with act.Fori(1, BATCH - 2, 2) as b:
                row(b, 1, True)
                row(b + 1, 0, True)
            row(BATCH - 1, 1, False)

        @block.tensor
        def _(pe):
            pe.wait_ge(s_const, 3)

            def ln_transposes(a, i):
                pe.wait_ge(s_staged, NG * a + i + 1)
                if i >= 2:
                    pe.wait_ge(s_lne, NG * a + i - 1)
                elif not first(a):
                    pe.wait_ge(s_qe, NJ * a)
                for k in range(4):
                    m = pe.transpose(ps_misc[i % 2][:, k * P:(k + 1) * P], stage[:, i % 2, k * P:(k + 1) * P],
                                     ident[:, :])
                m.then_inc(s_lnx, 1)

            def scores(a):
                pe.wait_ge(s_lne, NG * a + NG)
                pe.wait_ge(s_ctxt, 16 * a + 16)
                for t in range(TT):
                    for k in range(KD):
                        m = pe.matmul(ps_misc[0][:, t * SEQ:(t + 1) * SEQ], lnT[:, k, t * P:(t + 1) * P],
                                      ctxT[:, k, :], start=(k == 0), stop=(k == KD - 1))
                m.then_inc(s_score, 1)

            def attend(a, g):
                c, h = divmod(g, HALVES)
                if g == 0:
                    pe.wait_ge(s_prob, a + 1)
                    pe.wait_ge(s_ctx, 16 * a + 16)
                if g >= 2:
                    pe.wait_ge(s_x1, NG * a + g - 1)
                for t in range(TT):
                    m = pe.matmul(ps_misc[(g + 1) % 2][:, :], probs[:, t, c * P:(c + 1) * P],
                                  ctx_sb[:, t, h * 512:(h + 1) * 512], start=(t == 0), stop=(t == TT - 1))
                m.then_inc(s_att, 1)

            def q_transposes(a, j):
                pe.wait_ge(s_q, NJ * a + j + 1)
                if j >= 2:
                    pe.wait_ge(s_qe, NJ * a + j - 1)
                else:
                    pe.wait_ge(s_x1, NG * a + NG - 1 + j)
                for k in range(KD):
                    m = pe.transpose(ps_misc[(j + 1) % 2][:, :].bitcast(bf16)[:, k * P:(k + 1) * P],
                                     qrow[:, j % 2, k * P:(k + 1) * P], ident_b[:, :])
                m.then_inc(s_qx, 1)

            def product(b, p, w):
                if p == 0:
                    pe.wait_ge(s_qe, NJ * b + TT * (w + 1))
                if w == 0:
                    pe.wait_ge(s_wgu[p], 32)
                    if p >= 2 or not first(b):
                        pe.wait_ge(s_h, PAIRS * b + p - 1)
                wt, bank, done = ((w_gate, ps_gate, s_gate), (w_up, ps_up, s_up))[w]
                for i in range(2):
                    for k in range(KD):
                        m = pe.matmul(bank[p % 2][:, i * SEQ:(i + 1) * SEQ], wt[:, p, k, i * P:(i + 1) * P],
                                      qT[:, w, k, :], start=(k == 0), stop=(k == KD - 1))
                m.then_inc(done, 1)

            def down(b, g):
                t, h = divmod(g, HALVES)
                if g >= 2 or not first(b):
                    pe.wait_ge(s_out, NG * b + g - 1)
                for k in range(KI):
                    if g == 0 and k % 2 == 0:
                        pe.wait_ge(s_hq, PAIRS * b + k // 2 + 1)
                    if k == 0:
                        pe.wait_ge(s_wd[0], 16)
                    if k == KI // 2:
                        pe.wait_ge(s_wd[1], 32)
                    m = pe.matmul(ps_down[g % 2][:, :], hq[:, k, t * P:(t + 1) * P],
                                  w_down[:, k, h * 512:(h + 1) * 512], start=(k == 0), stop=(k == KI - 1))
                m.then_inc(s_down, 1)

            for i in range(NG):
                ln_transposes(0, i)
            scores(0)
            for g in range(NG):
                attend(0, g)
            for j in range(NJ):
                q_transposes(0, j)
            pe.wait_ge(s_pad, 3)

            def row(b, following):
                a = b + 1
                for p in range(PAIRS):
                    product(b, p, 0)
                    if following:
                        if p == 1:
                            ln_transposes(a, 0)
                            ln_transposes(a, 1)
                        if p == 4:
                            scores(a)
                        if p == 6:
                            attend(a, 2)
                            attend(a, 3)
                    product(b, p, 1)
                    if following:
                        if p == 3:
                            ln_transposes(a, 2)
                            ln_transposes(a, 3)
                        if p == 5:
                            attend(a, 0)
                            attend(a, 1)
                for g in range(NG):
                    down(b, g)
                    if following:
                        if g == 1:
                            q_transposes(a, 0)
                            q_transposes(a, 1)
                        if g == 2:
                            q_transposes(a, 2)
                if following:
                    q_transposes(a, 3)

            row(0, True)
            with pe.Fori(1, BATCH - 1) as b:
                row(b, True)
            row(BATCH - 1, False)

        @block.vector
        def _(dve):
            marks = [0]

            def mark(ins):
                marks[0] += 1
                ins.then_inc(s_dve, 1)
                return marks[0]

            def need(n):
                dve.wait_ge(s_dve, n)

            def fence():
                need(marks[0])
                dve.sem_clear(s_dve)
                marks[0] = 0

            dve.wait_ge(s_scal, 16)
            need(mark(dve.reciprocal(fac[:, 5:8], sc[:, 5:8])))
            dve.scalar_tensor_tensor(out=fac[:, 2:3], in0=sc[:, 2:3], scalar=-1.0, in1=sc[:, 5:6],
                                     op0=ALU.mult, op1=ALU.mult)
            need(mark(dve.scalar_tensor_tensor(out=fac[:, 3:4], in0=sc[:, 3:4], scalar=sc[:, 6:7], in1=fac[:, 7:8],
                                               op0=ALU.mult, op1=ALU.mult)))
            need(mark(dve.tensor_scalar(fac[:, 3:4], fac[:, 3:4], -1.0, None, ALU.mult)))
            dve.wait_ge(s_tanh, 1)
            dve.scalar_tensor_tensor(out=fac[:, 4:5], in0=sc[:, 4:5], scalar=sc[:, 7:8], in1=fac[:, 1:2],
                                     op0=ALU.mult, op1=ALU.mult).then_inc(s_fac, 1)
            dve.wait_ge(s_fac, 1)

            def tile_stats(t, h, odd):
                return mark(dve.bn_stats(stats[:, t, h, :], xs[odd][:, t, h * 512:(h + 1) * 512]))

            def aggregate(t):
                return mark(dve.bn_aggr(mv[:, t, :], stats[:, t, :, :].rearrange("p h s -> p (h s)")))

            def variance(t0, t1):
                dve.tensor_scalar(veps[:, t0:t1], mv[:, t0:t1, 1], EPS, None, ALU.add).then_inc(s_var, 1)

            def ln1_stats(a, t, odd):
                dve.wait_ge(s_x[odd][t], 8 * a + 16 - 8 * odd)
                for h in range(HALVES):
                    n = tile_stats(t, h, odd)
                need(n)
                need(aggregate(t))
                variance(t, t + 1)

            def norm1(a, t):
                dve.wait_ge(s_rstd, 3 * a + t + 1)
                dve.scalar_tensor_tensor(out=nm[:, t:t + 1], in0=mv[:, t:t + 1, 0], scalar=-1.0,
                                         in1=rstd[:, t:t + 1], op0=ALU.mult, op1=ALU.mult).then_inc(s_nm1, 1)

            def norm2(a):
                dve.wait_ge(s_rstd, 3 * a + TT + 1)
                for w in range(2):
                    n = mark(dve.tensor_scalar(rs2[:, w, :], rstd[:, :], fac[:, 5 + w:6 + w], None, ALU.mult))
                need(n)
                for w in range(2):
                    n = mark(dve.scalar_tensor_tensor(out=nm2[:, w, :], in0=mv[:, :, 0], scalar=-1.0,
                                                      in1=rs2[:, w, :], op0=ALU.mult, op1=ALU.mult))
                dve.tensor_scalar(rs2r[:, :, :], rs2[:, :, :], ROUND, None, ALU.mult)
                need(n)
                dve.tensor_scalar(nm2r[:, :, :], nm2[:, :, :], ROUND, None, ALU.mult).then_inc(s_nm2, 1)

            def maxima(a):
                dve.wait_ge(s_score, a + 1)
                need(mark(dve.reduce_max(mx[:, :], ps_misc[0][:, :].rearrange("p (t c) -> p t c", t=TT), AX.X)))
                dve.tensor_scalar(nmx[:, :], mx[:, :], -SCORE_SCALE, None, ALU.mult).then_inc(s_max, 1)

            def normalise(a):
                dve.wait_ge(s_exp, a + 1)
                need(mark(dve.reciprocal(rden[:, :], den[:, :])))
                for t in range(TT):
                    last = dve.tensor_scalar(probs[:, t, :], probs[:, t, :], rden[:, t:t + 1], None, ALU.mult)
                last.then_inc(s_prob, 1)

            def residual1(a, g, odd):
                c, h = divmod(g, HALVES)
                dve.wait_ge(s_att, NG * a + g + 1)
                at = xs[odd][:, c, h * 512:(h + 1) * 512]
                return dve.scalar_tensor_tensor(out=at, in0=ps_misc[(g + 1) % 2][:, :], scalar=fac[:, 0:1], in1=at,
                                                op0=ALU.mult, op1=ALU.add).then_inc(s_x1, 1)

            def attended(a, odd):
                n = [0] * TT
                for t in range(TT):
                    for h in range(HALVES):
                        residual1(a, t * HALVES + h, odd)
                    dve.wait_ge(s_x1, NG * a + HALVES * (t + 1))
                    for h in range(HALVES):
                        n[t] = tile_stats(t, h, odd)
                for t in range(TT):
                    need(n[t])
                    last = aggregate(t)
                need(last)
                variance(0, TT)

            at = {}

            def hidden_product(b, p):
                dve.wait_ge(s_silu, PAIRS * b + p + 1)
                dve.wait_ge(s_up, PAIRS * b + p + 1)
                v = act_sb[:, p % 2, :]
                dve.scalar_tensor_tensor(out=v, in0=ps_up[p % 2][:, :], scalar=fac[:, 3:4], in1=v,
                                         op0=ALU.mult, op1=ALU.mult).then_inc(s_h, 1)

            def hidden_exponent(b, p):
                dve.wait_ge(s_h, PAIRS * b + p + 1)
                high = act_sb[:, p % 2, :].bitcast(u16).rearrange("p (n two) -> p n two", two=2)[:, :, 1]
                at["exponent"] = mark(dve.tensor_scalar(hmag[:, p % 2, :].bitcast(u16), high, 0x7F80, 0x0040,
                                                        ALU.bitwise_and, ALU.bitwise_or))

            def hidden_range(p):
                need(at["exponent"])
                m = hmag[:, p % 2, :]
                at["magnitude"] = mark(dve.tensor_scalar(m, m, 1.5 * MIN_NORMAL, 1.5 * 2.0 ** 8, ALU.max, ALU.min))

            def hidden_add(p):
                need(at["magnitude"])
                v = act_sb[:, p % 2, :]
                at["sum"] = mark(dve.scalar_tensor_tensor(out=v, in0=hmag[:, p % 2, :], scalar=ROUND, in1=v,
                                                          op0=ALU.mult, op1=ALU.add))

            def hq_pair(p):
                return hq[:, 2 * p:2 * p + 2, :].rearrange("p a n -> p (a n)")

            def hidden_subtract(b, p):
                if p == 0 and not first(b):
                    dve.wait_ge(s_down, NG * b)
                need(at["sum"])
                at["rounded"] = mark(dve.scalar_tensor_tensor(out=hq_pair(p), in0=hmag[:, p % 2, :], scalar=-ROUND,
                                                              in1=act_sb[:, p % 2, :], op0=ALU.mult, op1=ALU.add))

            def hidden_clip(p):
                need(at["rounded"])
                dve.tensor_scalar(hq_pair(p), hq_pair(p), FP8_MAX, -FP8_MAX, ALU.min, ALU.max).then_inc(s_hq, 1)

            row_at = {}

            def row_exponent(a, j):
                dve.wait_ge(s_zmag, NJ * a + j + 1)
                m = zmag[:, j % 2, :].bitcast(u16)
                row_at["exponent", j] = mark(dve.tensor_scalar(m, m, 0x7F80, 0x0040, ALU.bitwise_and, ALU.bitwise_or))

            def row_add(a, j):
                dve.wait_ge(s_z, NJ * a + j + 1)
                need(row_at["exponent", j])
                v = z[:, j % 2, :]
                row_at["sum", j] = mark(dve.scalar_tensor_tensor(
                    out=v, in0=zmag[:, j % 2, :], scalar=1.5 * MIN_NORMAL * ROUND, in1=v, op0=ALU.max, op1=ALU.add))

            def row_subtract(a, j):
                if j >= 2:
                    dve.wait_ge(s_qx, NJ * a + j - 1)
                need(row_at["sum", j])
                row_at["rounded", j] = mark(dve.scalar_tensor_tensor(
                    out=qrow[:, j % 2, :], in0=zmag[:, j % 2, :], scalar=1.5 * MIN_NORMAL * ROUND, in1=z[:, j % 2, :],
                    op0=ALU.max, op1=ALU.subtract))

            def row_clip(j):
                need(row_at["rounded", j])
                dve.tensor_scalar(qrow[:, j % 2, :], qrow[:, j % 2, :], FP8_MAX, -FP8_MAX, ALU.min, ALU.max)\
                    .then_inc(s_q, 1)

            def residual2(b, g, odd):
                t, h = divmod(g, HALVES)
                dve.wait_ge(s_down, NG * b + g + 1)
                at = xs[odd][:, t, h * 512:(h + 1) * 512]
                dve.scalar_tensor_tensor(out=at, in0=ps_down[g % 2][:, :], scalar=fac[:, 4:5], in1=at,
                                         op0=ALU.mult, op1=ALU.add).then_inc(s_out, 1)

            for t in range(TT):
                ln1_stats(0, t, 0)
            for t in range(TT):
                norm1(0, t)
            maxima(0)
            normalise(0)
            attended(0, 0)
            norm2(0)
            row_exponent(0, 0)
            row_add(0, 0)
            row_exponent(0, 1)
            row_subtract(0, 0)
            row_add(0, 1)
            row_clip(0)
            row_subtract(0, 1)
            row_exponent(0, 2)
            row_clip(1)
            row_add(0, 2)
            row_exponent(0, 3)
            row_subtract(0, 2)
            row_add(0, 3)
            row_clip(2)
            row_subtract(0, 3)
            row_clip(3)

            def row(b, odd, following):
                fence()
                a = b + 1
                for p in range(PAIRS):
                    if following:
                        if p == 0:
                            ln1_stats(a, 0, 1 - odd)
                            norm1(a, 0)
                        if p == 4:
                            maxima(a)
                        if p == 6:
                            attended(a, 1 - odd)
                    hidden_product(b, p)
                    if p >= 1:
                        hidden_subtract(b, p - 1)
                    hidden_exponent(b, p)
                    if p >= 1:
                        hidden_clip(p - 1)
                    hidden_range(p)
                    if following:
                        if p == 1:
                            ln1_stats(a, 1, 1 - odd)
                        if p == 2:
                            norm1(a, 1)
                        if p == 6:
                            norm2(a)
                        if p == 4:
                            normalise(a)
                        if p == 8:
                            row_exponent(a, 0)
                        if p == 9:
                            row_add(a, 0)
                        if p == 10:
                            row_exponent(a, 1)
                    hidden_add(p)
                    if following and p == 9:
                        row_subtract(a, 0)
                if following:
                    row_clip(0)
                hidden_subtract(b, PAIRS - 1)
                hidden_clip(PAIRS - 1)
                if following:
                    row_add(a, 1)
                    row_subtract(a, 1)
                    row_exponent(a, 2)
                    row_clip(1)
                residual2(b, 0, odd)
                if following:
                    row_add(a, 2)
                    row_exponent(a, 3)
                    row_subtract(a, 2)
                residual2(b, 1, odd)
                if following:
                    row_add(a, 3)
                    row_clip(2)
                    row_subtract(a, 3)
                    row_clip(3)
                residual2(b, 2, odd)
                residual2(b, 3, odd)

            row(0, 0, True)
            with dve.Fori(1, BATCH - 2, 2) as b:
                row(b, 1, True)
                row(b + 1, 0, True)
            row(BATCH - 1, 1, False)


def kernel(x, ctx_4096, g_xattn, g_ffn, L0_ffn_gate_w, L0_ffn_up_w, L0_ffn_down_w, L0_ffn_gate_w_scale,
           L0_ffn_up_w_scale, L0_ffn_down_w_scale, L0_ffn_gate_in_scale, L0_ffn_up_in_scale, L0_ffn_down_in_scale):
    import numpy as np
    import concourse.bacc as bacc
    from concourse.bass_utils import run_bass_kernel_spmd

    def up_pairs(w):
        w = np.asarray(w)
        main = w[:FULL * 256].reshape(FULL, 256, KD, P).transpose(3, 0, 2, 1)
        tail = w[FULL * 256:].reshape(TAIL, KD, P).transpose(2, 1, 0)
        return np.ascontiguousarray(main), np.ascontiguousarray(tail)

    gate_main, gate_tail = up_pairs(L0_ffn_gate_w)
    up_main, up_tail = up_pairs(L0_ffn_up_w)
    down = np.asarray(L0_ffn_down_w)
    down_main = np.ascontiguousarray(down[:, :(KI - 1) * P].reshape(DIM, KI - 1, P).transpose(2, 1, 0))
    down_tail = np.ascontiguousarray(down[:, (KI - 1) * P:].transpose(1, 0))
    ctx = np.ascontiguousarray(np.asarray(ctx_4096))
    ctx_t = np.ascontiguousarray(ctx.reshape(BATCH, SEQ, KD, P).transpose(0, 3, 2, 1))
    scalars = np.concatenate([np.asarray(s).reshape(1, 1) for s in (
        g_xattn, g_ffn, L0_ffn_gate_w_scale, L0_ffn_up_w_scale, L0_ffn_down_w_scale,
        L0_ffn_gate_in_scale, L0_ffn_up_in_scale, L0_ffn_down_in_scale)], axis=1)

    nc = bacc.Bacc("TRN2", target_bir_lowering=False, num_devices=1)
    arrays, args = {}, []
    for name, a in (("x", np.ascontiguousarray(np.asarray(x))), ("ctx", ctx), ("ctx_t", ctx_t), ("scalars", scalars),
                    ("gate_main", gate_main), ("gate_tail", gate_tail), ("up_main", up_main),
                    ("up_tail", up_tail), ("down_main", down_main), ("down_tail", down_tail)):
        arrays[name] = a
        args.append(nc.dram_tensor(name, a.shape, mybir.dt.from_np(a.dtype), kind="ExternalInput").ap())
    args.append(nc.dram_tensor("out", (BATCH, SEQ, DIM), mybir.dt.float32, kind="ExternalOutput").ap())
    gated_xattn_ffn(nc, *args)
    r = run_bass_kernel_spmd(nc, [arrays], core_ids=[0])
    return r.results[0]["out"]
```

```python
from contextlib import ExitStack

import concourse.bass as bass
from concourse import mybir

P = 128
BATCH, SEQ, DIM, INNER = 8, 256, 1024, 2752
TT = SEQ // P
KD = DIM // P
HALVES = DIM // 512
PAIRS = -(-INNER // 256)
KI = 2 * PAIRS
TAIL = INNER - (PAIRS - 1) * 256
DTAIL = INNER - (KI - 1) * P
FULL = PAIRS - 1
EPS = 1e-5
FP8_MAX = 448.0
MIN_NORMAL = 2.0 ** -6
ROUND = 2.0 ** 20
SCORE_SCALE = float(SEQ) ** -0.5
WARM = (56, 20, 20, 150, 20, 36)


def gated_xattn_ffn(nc, x, x_t, ctx, ctx_t, scalars, gate_main, gate_tail, up_main, up_tail,
                    down_main, down_tail, out):
    f32, bf16, u16 = mybir.dt.float32, mybir.dt.bfloat16, mybir.dt.uint16
    ALU, ACT, AX = mybir.AluOpType, mybir.ActivationFunctionType, mybir.AxisListType

    es = ExitStack()
    with es:
        def sb(name, shape, dt):
            return es.enter_context(nc.sbuf_tensor(name, shape, dt))

        def ps(name):
            return es.enter_context(nc.psum_tensor(name, [P, 512], f32))

        def sem(name):
            return es.enter_context(nc.semaphore(name))

        w_gate = sb("w_gate", [P, PAIRS, KD, 256], bf16)
        w_up = sb("w_up", [P, PAIRS, KD, 256], bf16)
        w_down = sb("w_down", [P, KI, DIM], bf16)
        z_row0 = w_down[:, 0:8, :].rearrange("p k n -> p (k n)").bitcast(f32).rearrange("p (s n) -> p s n", n=DIM)
        zmag_row0 = w_down[:, 8:12, :]
        hq = sb("hq", [P, KI, SEQ], bf16)
        qT = sb("qT", [P, 2, KD, SEQ], bf16)
        xs = [sb(f"x_row{i}", [P, TT, DIM], f32) for i in range(2)]
        ctx_sb = sb("ctx_sb", [P, TT, DIM], f32)
        ctxT = sb("ctxT", [P, KD, SEQ], f32)
        xT = sb("xT", [P, KD, SEQ], f32)
        z = xT[:, :, :].rearrange("p (s a) n -> p s (a n)", s=2)
        qrow = sb("qrow", [P, 2, DIM], bf16)
        probs = qrow[:, 1, :].bitcast(f32).rearrange("p (t c) -> p t c", t=TT)
        zmag = sb("zmag", [P, 2, DIM], bf16)
        act_sb = sb("act_sb", [P, 2, 512], f32)
        hmag = sb("hmag", [P, 2, 512], bf16)
        ident = sb("ident", [P, P], f32)
        ident_b = sb("ident_b", [P, P], bf16)
        sc = sb("sc", [P, 8], f32)
        fac = sb("fac", [P, 8], f32)
        stats = sb("stats", [P, TT, HALVES, 6], f32)
        mv = sb("mv", [P, TT, 2], f32)
        veps = sb("veps", [P, TT], f32)
        rstd = sb("rstd", [P, TT], f32)
        nhalf = sb("nhalf", [P, TT], f32)
        means = sb("means", [P, TT, P], f32)
        srstd = sb("srstd", [P, TT], f32)
        rs2 = sb("rs2", [P, TT, 2], f32)
        nm2 = sb("nm2", [P, TT, 2], f32)
        rs2r = sb("rs2r", [P, TT, 2], f32)
        nm2r = sb("nm2r", [P, TT, 2], f32)
        mx = sb("mx", [P, TT], f32)
        nmx = sb("nmx", [P, TT], f32)
        den = sb("den", [P, TT], f32)
        rden = sb("rden", [P, TT], f32)

        ps_gate = [ps("ps_gate0"), ps("ps_gate1")]
        ps_up = [ps("ps_up0"), ps("ps_up1")]
        ps_down = [ps("ps_down0"), ps("ps_down1")]
        ps_misc = [ps("ps_misc0"), ps("ps_misc1")]

        s_scal = sem("scalars_loaded")
        s_x = [[sem(f"x_loaded{i}_{t}") for t in range(TT)] for i in range(2)]
        s_xt = sem("xT_loaded")
        s_ctx = sem("ctx_loaded")
        s_ctxt = [sem(f"ctxT_loaded{h}") for h in range(2)]
        s_wgu = [sem(f"gate_up_weights{p}") for p in range(PAIRS)]
        s_wd = [sem(f"down_weights{h}") for h in range(2)]
        s_store = [sem(f"out_stored{t}") for t in range(TT)]
        s_pad = sem("padding_zeroed")
        s_ident = sem("identity_zeroed")
        s_const = sem("constants_ready")
        s_tanh = sem("tanh_ready")
        s_fac = sem("factors_ready")
        s_var = sem("variance_ready")
        s_rstd = sem("rstd_ready")
        s_copied = sem("means_copied")
        s_mean = sem("means_transposed")
        s_centred = sem("xT_centred")
        s_score = sem("scores_done")
        s_max = sem("max_ready")
        s_exp = sem("exp_done")
        s_prob = sem("probs_ready")
        s_att = sem("attended")
        s_x1 = sem("x1_ready")
        s_nm2 = sem("norm2_ready")
        s_zmag = sem("scaled_z_ready")
        s_z = sem("z_ready")
        s_q = sem("q_ready")
        s_qx = sem("q_transposed")
        s_qe = sem("qT_written")
        s_gate = sem("gate_done")
        s_up = sem("up_done")
        s_silu = sem("silu_done")
        s_h = sem("hidden_made")
        s_hq = sem("hidden_quantised")
        s_down = sem("down_done")
        s_out = sem("out_ready")
        s_dve = sem("dve_chain")

        NG = TT * HALVES
        NJ = 2 * TT

        def first(b):
            return isinstance(b, int) and b == 0

        def z_slot(a, j):
            return z_row0[:, j, :] if first(a) else z[:, j % 2, :]

        def zmag_slot(a, j):
            return zmag_row0[:, j, :] if first(a) else zmag[:, j % 2, :]

        block = es.enter_context(nc.Block())

        @block.sync
        def _(sp):
            sp.dma_start(sc[:, :], scalars.to_broadcast([P, 8])).then_inc(s_scal, 16)

            def load_x(a, t, odd):
                sp.dma_start(xs[odd][:, t, :], x[bass.ds(a, 1), t * P:(t + 1) * P, :].rearrange("o p n -> p (o n)"))\
                    .then_inc(s_x[odd][t], 16)

            def load_xt(a):
                sp.dma_start(xT[:, :, :], x_t[bass.ds(a, 1), :, :, :].rearrange("o p k n -> p (o k) n"))\
                    .then_inc(s_xt, 16)

            def load_ctxt(a):
                for h in range(2):
                    ks = slice(4 * h, 4 * h + 4)
                    sp.dma_start(ctxT[:, ks, :], ctx_t[bass.ds(a, 1), :, ks, :].rearrange("o p k n -> p (o k) n"))\
                        .then_inc(s_ctxt[h], 16)

            def load_ctx(a):
                sp.dma_start(ctx_sb[:, :, :], ctx[bass.ds(a, 1), :, :].rearrange("o (t p) n -> p (o t) n", p=P))\
                    .then_inc(s_ctx, 16)

            def store(b, t, odd):
                sp.wait_ge(s_out, NG * b + HALVES * (t + 1))
                sp.dma_start(out[bass.ds(b, 1), t * P:(t + 1) * P, :].rearrange("o p n -> p (o n)"), xs[odd][:, t, :])\
                    .then_inc(s_store[t], 16)

            def store_half(b, g, odd):
                t, h = divmod(g, HALVES)
                sp.wait_ge(s_out, NG * b + g + 1)
                sp.dma_start(out[b, t * P:(t + 1) * P, h * 512:(h + 1) * 512], xs[odd][:, t, h * 512:(h + 1) * 512])\
                    .then_inc(s_store[t], 16)

            def row(b, odd, following):
                if following:
                    sp.wait_ge(s_score, TT * b + 2 * TT)
                    load_ctxt(b + 2)
                    sp.wait_ge(s_att, NG * b + 2 * NG)
                    load_ctx(b + 2)
                for t in range(TT):
                    store(b, t, odd)
                    if following and t == 0:
                        sp.wait_ge(s_q, NJ * b + 2 * NJ)
                        load_xt(b + 2)
                    if following:
                        sp.wait_ge(s_store[t], 16 * b + 16)
                        load_x(b + 2, t, odd)

            for t in range(TT):
                load_x(0, t, 0)
            load_xt(0)
            load_ctxt(0)
            load_ctx(0)
            for t in range(TT):
                load_x(1, t, 1)
            sp.wait_ge(s_score, TT)
            load_xt(1)
            load_ctxt(1)
            sp.wait_ge(s_att, NG)
            load_ctx(1)
            with sp.Fori(0, BATCH - 3, 2) as b:
                row(b, 0, True)
                row(b + 1, 1, True)
            row(BATCH - 2, 0, False)
            for g in range(NG):
                store_half(BATCH - 1, g, 1)
            for t in range(TT):
                sp.wait_ge(s_store[t], 16 * (BATCH - 1 + HALVES))

        @block.gpsimd
        def _(pool):
            pool.memset(w_down[DTAIL:P, KI - 1, :], 0.0).then_inc(s_pad, 1)
            pool.wait_ge(s_pad, 1)
            pool.memset(nhalf[:, :], -0.5).then_inc(s_const, 1)
            pool.memset(ident[:, :], 0.0).then_inc(s_ident, 1)
            pool.memset(ident_b[:, :], 0.0).then_inc(s_ident, 1)
            pool.wait_ge(s_const, 1)
            pool.wait_ge(s_ident, 2)
            for m in (ident, ident_b):
                pool.affine_select(out=m[:, :], in_=m[:, :], compare_op=ALU.not_equal, fill=1.0,
                                   base=0, pattern=[[-1, P]], channel_multiplier=1).then_inc(s_const, 1)

            def inverse_root(n, t):
                pool.wait_ge(s_var, n + 1)
                pool.tensor_tensor(rstd[:, t:t + 1], veps[:, t:t + 1], nhalf[:, t:t + 1], ALU.pow)\
                    .then_inc(s_rstd, 1)

            def load_pair(p):
                pool.dma_start(w_gate[:, p, :, :], gate_main[:, p, :, :]).then_inc(s_wgu[p], 16)
                pool.dma_start(w_up[:, p, :, :], up_main[:, p, :, :]).then_inc(s_wgu[p], 16)

            load_pair(0)
            load_pair(1)
            for t in range(TT):
                inverse_root(t, t)
            for p in range(2, FULL - 2):
                load_pair(p)
            for t in range(TT):
                inverse_root(TT + t, t)
            for p in range(FULL - 2, FULL):
                load_pair(p)
            pool.dma_start(w_gate[:, FULL, :, 0:TAIL], gate_tail).then_inc(s_wgu[FULL], 16)
            pool.dma_start(w_up[:, FULL, :, 0:TAIL], up_tail).then_inc(s_wgu[FULL], 16)
            half = KI // 2
            pool.wait_ge(s_q, NJ)
            pool.dma_start(w_down[:, 0:half, :], down_main[:, 0:half, :]).then_inc(s_wd[0], 16)
            pool.dma_start(w_down[:, half:KI - 1, :], down_main[:, half:KI - 1, :]).then_inc(s_wd[1], 16)
            pool.dma_start(w_down[0:DTAIL, KI - 1, :], down_tail).then_inc(s_wd[1], 16)
            with pool.Fori(1, BATCH) as a:
                for n in range(2 * TT):
                    inverse_root(2 * TT * a + n, n % TT)

        @block.scalar
        def _(act):
            act.wait_ge(s_scal, 16)
            act.activation(fac[:, 0:2], sc[:, 0:2], ACT.Tanh).then_inc(s_tanh, 1)

            def exps(a):
                for t in range(TT):
                    act.wait_ge(s_max, TT * a + t + 1)
                    act.activation(probs[:, t, :], ps_misc[t][:, 0:SEQ], ACT.Exp, bias=nmx[:, t:t + 1],
                                   scale=srstd[:, t:t + 1], accum_out=den[:, t:t + 1]).then_inc(s_exp, 1)

            def make_z(a, j, odd):
                w, t = divmod(j, TT)
                if w == 0:
                    act.wait_ge(s_nm2, TT * a + t + 1)
                if j >= 2 and not first(a):
                    act.wait_ge(s_q, NJ * a + j - 1)
                act.activation(zmag_slot(a, j), xs[odd][:, t, :], ACT.Identity,
                               bias=nm2r[:, t, w:w + 1], scale=rs2r[:, t, w:w + 1]).then_inc(s_zmag, 1)
                act.activation(z_slot(a, j), xs[odd][:, t, :], ACT.Identity,
                               bias=nm2[:, t, w:w + 1], scale=rs2[:, t, w:w + 1]).then_inc(s_z, 1)

            def q_evac(a, j):
                w, t = divmod(j, TT)
                act.wait_ge(s_qx, NJ * a + j + 1)
                act.activation(qT[:, w, :, t * P:(t + 1) * P],
                               ps_misc[(j + 1) % 2][:, :].bitcast(bf16).rearrange("p (k n) -> p k n", n=P), ACT.Copy)\
                    .then_inc(s_qe, 1)

            def silu(b, p):
                act.wait_ge(s_gate, PAIRS * b + p + 1)
                if p >= 2 or not first(b):
                    act.wait_ge(s_hq, PAIRS * b + p - 1)
                if p < FULL:
                    act.activation(act_sb[:, p % 2, :], ps_gate[p % 2][:, :], ACT.Silu,
                                   scale=fac[:, 2:3]).then_inc(s_silu, 1)
                else:
                    act.activation(act_sb[:, p % 2, 0:SEQ], ps_gate[p % 2][:, 0:SEQ], ACT.Silu, scale=fac[:, 2:3])
                    act.activation(act_sb[0:DTAIL, p % 2, SEQ:2 * SEQ], ps_gate[p % 2][0:DTAIL, SEQ:2 * SEQ],
                                   ACT.Silu, scale=fac[0:DTAIL, 2:3]).then_inc(s_silu, 1)

            exps(0)
            for j in range(NJ):
                make_z(0, j, 0)
            q_evac(0, 0)
            q_evac(0, 1)
            act.wait_ge(s_fac, 1)

            def row(b, odd, following):
                a = b + 1
                for p in range(PAIRS):
                    if following:
                        if p == 5:
                            exps(a)
                        if p == 8:
                            make_z(a, 0, 1 - odd)
                        if p == 9:
                            make_z(a, 1, 1 - odd)
                    if p == 0 and first(b):
                        q_evac(b, 2)
                        q_evac(b, 3)
                    silu(b, p)
                if following:
                    make_z(a, 2, 1 - odd)
                    make_z(a, 3, 1 - odd)
                    q_evac(a, 0)
                    q_evac(a, 1)
                    q_evac(a, 2)
                    q_evac(a, 3)

            row(0, 0, True)
            with act.Fori(1, BATCH - 2, 2) as b:
                row(b, 1, True)
                row(b + 1, 0, True)
            row(BATCH - 1, 1, False)

        @block.tensor
        def _(pe):
            pe.wait_ge(s_const, 3)

            def transpose_means(a):
                pe.wait_ge(s_copied, TT * a + TT)
                if not first(a):
                    pe.wait_ge(s_qe, NJ * a)
                for t in range(TT):
                    m = pe.transpose(ps_misc[1][:, t * P:(t + 1) * P], means[:, t, :], ident[:, :])
                m.then_inc(s_mean, 1)

            def scores(a):
                for t in range(TT):
                    for k in range(KD):
                        if t == 0 and k % 4 == 0:
                            pe.wait_ge(s_centred, NG * a + k // 4 + 1)
                            pe.wait_ge(s_ctxt[k // 4], 16 * a + 16)
                        if t == 1 and k == 0:
                            pe.wait_ge(s_centred, NG * a + NG)
                        m = pe.matmul(ps_misc[t][:, 0:SEQ], xT[:, k, t * P:(t + 1) * P],
                                      ctxT[:, k, :], start=(k == 0), stop=(k == KD - 1))
                    m.then_inc(s_score, 1)

            def keep_warm(n):
                for _ in range(n):
                    pe.matmul(ps_down[0][:, 0:P], ident_b[:, :], ident_b[:, :], start=True, stop=True)

            def attend(a, g):
                c, h = divmod(g, HALVES)
                if g == 0:
                    pe.wait_ge(s_prob, a + 1)
                    pe.wait_ge(s_ctx, 16 * a + 16)
                if g >= 2:
                    pe.wait_ge(s_x1, NG * a + g - 1)
                for t in range(TT):
                    m = pe.matmul(ps_misc[(g + 1) % 2][:, :], probs[:, t, c * P:(c + 1) * P],
                                  ctx_sb[:, t, h * 512:(h + 1) * 512], start=(t == 0), stop=(t == TT - 1))
                m.then_inc(s_att, 1)

            def q_transposes(a, j):
                pe.wait_ge(s_q, NJ * a + j + 1)
                if j >= 2:
                    pe.wait_ge(s_qe, NJ * a + j - 1)
                else:
                    pe.wait_ge(s_x1, NG * a + NG - 1 + j)
                for k in range(KD):
                    m = pe.transpose(ps_misc[(j + 1) % 2][:, :].bitcast(bf16)[:, k * P:(k + 1) * P],
                                     qrow[:, j % 2, k * P:(k + 1) * P], ident_b[:, :])
                m.then_inc(s_qx, 1)

            def product(b, p, w):
                if p == 0:
                    pe.wait_ge(s_qe, NJ * b + TT * (w + 1))
                if w == 0:
                    pe.wait_ge(s_wgu[p], 32)
                    if p >= 2 or not first(b):
                        pe.wait_ge(s_h, PAIRS * b + p - 1)
                wt, bank, done = ((w_gate, ps_gate, s_gate), (w_up, ps_up, s_up))[w]
                for i in range(2 if p < FULL else 1):
                    for k in range(KD):
                        m = pe.matmul(bank[p % 2][:, i * SEQ:(i + 1) * SEQ], wt[:, p, k, i * P:(i + 1) * P],
                                      qT[:, w, k, :], start=(k == 0), stop=(k == KD - 1))
                if p == FULL and w == 0:
                    for k in range(KD):
                        m = pe.matmul(ps_gate[p % 2][0:DTAIL, SEQ:2 * SEQ], w_gate[:, p, k, P:TAIL], qT[:, 0, k, :],
                                      start=(k == 0), stop=(k == KD - 1))
                        pe.matmul(ps_up[p % 2][DTAIL:2 * DTAIL, SEQ:2 * SEQ], w_up[:, p, k, P:TAIL], qT[:, 1, k, :],
                                  start=(k == 0), stop=(k == KD - 1))
                m.then_inc(done, 1)

            def down(b, g, k0, k1):
                t, h = divmod(g, HALVES)
                if k0 == 0 and (g >= 2 or not first(b)):
                    pe.wait_ge(s_out, NG * b + g - 1)
                for k in range(k0, k1):
                    if g == 0 and k % 2 == 0:
                        pe.wait_ge(s_hq, PAIRS * b + k // 2 + 1)
                    if g == 0 and k == 0:
                        pe.wait_ge(s_wd[0], 16)
                    if g == 0 and k == KI // 2:
                        pe.wait_ge(s_wd[1], 32)
                    m = pe.matmul(ps_down[g % 2][:, :], hq[:, k, t * P:(t + 1) * P],
                                  w_down[:, k, h * 512:(h + 1) * 512], start=(k == 0), stop=(k == KI - 1))
                if k1 == KI:
                    m.then_inc(s_down, 1)

            keep_warm(WARM[0])
            transpose_means(0)
            keep_warm(WARM[1])
            scores(0)
            keep_warm(WARM[2])
            for g in range(NG):
                attend(0, g)
            keep_warm(WARM[3])
            q_transposes(0, 0)
            keep_warm(WARM[4])
            q_transposes(0, 1)
            keep_warm(WARM[5])
            pe.wait_ge(s_pad, 1)

            def row(b, following):
                a = b + 1
                for p in range(PAIRS):
                    if p != 1 or not first(b):
                        product(b, p, 0)
                    if p == 0 and first(b):
                        q_transposes(b, 2)
                        product(b, 1, 0)
                        q_transposes(b, 3)
                    if following:
                        if p == 3:
                            transpose_means(a)
                        if p == 4:
                            scores(a)
                        if p == 6:
                            attend(a, 2)
                            attend(a, 3)
                    product(b, p, 1)
                    if following:
                        if p == 5:
                            attend(a, 0)
                            attend(a, 1)
                down(b, 0, 0, KI - 4)
                down(b, 1, 0, KI // 2)
                down(b, 0, KI - 4, KI)
                down(b, 1, KI // 2, KI)
                if following:
                    q_transposes(a, 0)
                    q_transposes(a, 1)
                down(b, 2, 0, KI)
                if following:
                    q_transposes(a, 2)
                down(b, 3, 0, KI)
                if following:
                    q_transposes(a, 3)

            row(0, True)
            with pe.Fori(1, BATCH - 1) as b:
                row(b, True)
            row(BATCH - 1, False)

        @block.vector
        def _(dve):
            marks = [0]

            def mark(ins):
                marks[0] += 1
                ins.then_inc(s_dve, 1)
                return marks[0]

            def need(n):
                dve.wait_ge(s_dve, n)

            def fence():
                need(marks[0])
                dve.sem_clear(s_dve)
                marks[0] = 0

            dve.wait_ge(s_const, 3)
            dve.wait_ge(s_scal, 16)
            need(mark(dve.reciprocal(fac[:, 5:8], sc[:, 5:8])))
            dve.scalar_tensor_tensor(out=fac[:, 2:3], in0=sc[:, 2:3], scalar=-1.0, in1=sc[:, 5:6],
                                     op0=ALU.mult, op1=ALU.mult)
            need(mark(dve.scalar_tensor_tensor(out=fac[:, 3:4], in0=sc[:, 3:4], scalar=sc[:, 6:7], in1=fac[:, 7:8],
                                               op0=ALU.mult, op1=ALU.mult)))
            need(mark(dve.tensor_scalar(fac[:, 3:4], fac[:, 3:4], -1.0, None, ALU.mult)))
            dve.wait_ge(s_tanh, 1)
            dve.scalar_tensor_tensor(out=fac[:, 4:5], in0=sc[:, 4:5], scalar=sc[:, 7:8], in1=fac[:, 1:2],
                                     op0=ALU.mult, op1=ALU.mult).then_inc(s_fac, 1)
            dve.wait_ge(s_fac, 1)

            def tile_stats(t, h, odd):
                return mark(dve.bn_stats(stats[:, t, h, :], xs[odd][:, t, h * 512:(h + 1) * 512]))

            def aggregate(t):
                return mark(dve.bn_aggr(mv[:, t, :], stats[:, t, :, :].rearrange("p h s -> p (h s)")))

            def variance(t):
                dve.tensor_scalar(veps[:, t:t + 1], mv[:, t:t + 1, 1], EPS, None, ALU.add).then_inc(s_var, 1)

            def ln1_stats(a, t, odd):
                dve.wait_ge(s_x[odd][t], 8 * a + 16 - 8 * odd)
                for h in range(HALVES):
                    n = tile_stats(t, h, odd)
                need(n)
                need(aggregate(t))
                variance(t)
                dve.tensor_scalar(means[:, t, :], ident[:, :], 0.0, mv[:, t:t + 1, 0], ALU.mult, ALU.add)\
                    .then_inc(s_copied, 1)

            def norm1(a):
                dve.wait_ge(s_rstd, 2 * TT * a + TT)
                return mark(dve.tensor_scalar(srstd[:, :], rstd[:, :], SCORE_SCALE, None, ALU.mult))

            def centre(a, t):
                if t == 0:
                    dve.wait_ge(s_mean, a + 1)
                    dve.wait_ge(s_xt, 16 * a + 16)
                for h in range(2):
                    at = xT[:, 4 * h:4 * h + 4, t * P:(t + 1) * P]
                    mean = ps_misc[1][:, t * P:(t + 1) * P].rearrange("p (o n) -> p o n", o=1).to_broadcast([P, 4, P])
                    dve.tensor_tensor(at, at, mean, ALU.subtract).then_inc(s_centred, 1)

            def norm2(a, t):
                dve.wait_ge(s_rstd, 2 * TT * a + TT + t + 1)
                n = mark(dve.tensor_scalar(rs2[:, t, :], fac[:, 5:7], rstd[:, t:t + 1], None, ALU.mult))
                need(n)
                n = mark(dve.tensor_scalar(nm2[:, t, :], rs2[:, t, :], mv[:, t:t + 1, 0], -1.0, ALU.mult, ALU.mult))
                dve.tensor_scalar(rs2r[:, t, :], rs2[:, t, :], ROUND, None, ALU.mult)
                need(n)
                dve.tensor_scalar(nm2r[:, t, :], nm2[:, t, :], ROUND, None, ALU.mult).then_inc(s_nm2, 1)

            def maxima(a, t):
                dve.wait_ge(s_score, TT * a + t + 1)
                need(mark(dve.reduce_max(mx[:, t:t + 1], ps_misc[t][:, 0:SEQ], AX.X)))
                dve.scalar_tensor_tensor(out=nmx[:, t:t + 1], in0=mx[:, t:t + 1], scalar=-1.0, in1=srstd[:, t:t + 1],
                                         op0=ALU.mult, op1=ALU.mult).then_inc(s_max, 1)

            def normalise(a, t):
                dve.wait_ge(s_exp, TT * a + t + 1)
                need(mark(dve.reciprocal(rden[:, t:t + 1], den[:, t:t + 1])))
                last = dve.tensor_scalar(probs[:, t, :], probs[:, t, :], rden[:, t:t + 1], None, ALU.mult)
                if t == TT - 1:
                    last.then_inc(s_prob, 1)

            def residual1(a, g, odd):
                c, h = divmod(g, HALVES)
                dve.wait_ge(s_att, NG * a + g + 1)
                at = xs[odd][:, c, h * 512:(h + 1) * 512]
                return dve.scalar_tensor_tensor(out=at, in0=ps_misc[(g + 1) % 2][:, :], scalar=fac[:, 0:1], in1=at,
                                                op0=ALU.mult, op1=ALU.add).then_inc(s_x1, 1)

            def x1_stats(a, t, odd):
                dve.wait_ge(s_x1, NG * a + HALVES * (t + 1))
                for h in range(HALVES):
                    n = tile_stats(t, h, odd)
                need(n)
                need(aggregate(t))
                variance(t)

            at = {}

            def hidden_product(b, p):
                dve.wait_ge(s_silu, PAIRS * b + p + 1)
                dve.wait_ge(s_up, PAIRS * b + p + 1)
                if p < FULL:
                    v = act_sb[:, p % 2, :]
                    dve.scalar_tensor_tensor(out=v, in0=ps_up[p % 2][:, :], scalar=fac[:, 3:4], in1=v,
                                             op0=ALU.mult, op1=ALU.mult).then_inc(s_h, 1)
                else:
                    v = act_sb[:, p % 2, 0:SEQ]
                    dve.scalar_tensor_tensor(out=v, in0=ps_up[p % 2][:, 0:SEQ], scalar=fac[:, 3:4], in1=v,
                                             op0=ALU.mult, op1=ALU.mult)
                    v = act_sb[0:DTAIL, p % 2, SEQ:2 * SEQ]
                    dve.scalar_tensor_tensor(out=v, in0=ps_up[p % 2][DTAIL:2 * DTAIL, SEQ:2 * SEQ],
                                             scalar=fac[0:DTAIL, 3:4], in1=v, op0=ALU.mult, op1=ALU.mult)\
                        .then_inc(s_h, 1)

            def hidden_exponent(b, p):
                dve.wait_ge(s_h, PAIRS * b + p + 1)
                high = act_sb[:, p % 2, :].bitcast(u16).rearrange("p (n two) -> p n two", two=2)[:, :, 1]
                at["exponent"] = mark(dve.tensor_scalar(hmag[:, p % 2, :].bitcast(u16), high, 0x7F80, 0x0040,
                                                        ALU.bitwise_and, ALU.bitwise_or))

            def hidden_range(p):
                need(at["exponent"])
                m = hmag[:, p % 2, :]
                at["magnitude"] = mark(dve.tensor_scalar(m, m, 1.5 * MIN_NORMAL, 1.5 * 2.0 ** 8, ALU.max, ALU.min))

            def hidden_add(p):
                need(at["magnitude"])
                v = act_sb[:, p % 2, :]
                at["sum"] = mark(dve.scalar_tensor_tensor(out=v, in0=hmag[:, p % 2, :], scalar=ROUND, in1=v,
                                                          op0=ALU.mult, op1=ALU.add))

            def hq_pair(p):
                return hq[:, 2 * p:2 * p + 2, :].rearrange("p a n -> p (a n)")

            def hidden_subtract(b, p):
                if p == 0 and not first(b):
                    dve.wait_ge(s_down, NG * b)
                need(at["sum"])
                at["rounded"] = mark(dve.scalar_tensor_tensor(out=hq_pair(p), in0=hmag[:, p % 2, :], scalar=-ROUND,
                                                              in1=act_sb[:, p % 2, :], op0=ALU.mult, op1=ALU.add))

            def hidden_clip(p):
                need(at["rounded"])
                dve.tensor_scalar(hq_pair(p), hq_pair(p), FP8_MAX, -FP8_MAX, ALU.min, ALU.max).then_inc(s_hq, 1)

            row_at = {}

            def row_exponent(a, j):
                dve.wait_ge(s_zmag, NJ * a + j + 1)
                m = zmag_slot(a, j).bitcast(u16)
                row_at["exponent", j] = mark(dve.tensor_scalar(m, m, 0x7F80, 0x0040, ALU.bitwise_and, ALU.bitwise_or))

            def row_add(a, j):
                dve.wait_ge(s_z, NJ * a + j + 1)
                need(row_at["exponent", j])
                v = z_slot(a, j)
                row_at["sum", j] = mark(dve.scalar_tensor_tensor(
                    out=v, in0=zmag_slot(a, j), scalar=1.5 * MIN_NORMAL * ROUND, in1=v, op0=ALU.max, op1=ALU.add))

            def row_subtract(a, j):
                if j >= 2:
                    dve.wait_ge(s_qx, NJ * a + j - 1)
                need(row_at["sum", j])
                row_at["rounded", j] = mark(dve.scalar_tensor_tensor(
                    out=qrow[:, j % 2, :], in0=zmag_slot(a, j), scalar=1.5 * MIN_NORMAL * ROUND, in1=z_slot(a, j),
                    op0=ALU.max, op1=ALU.subtract))

            def row_clip(j):
                need(row_at["rounded", j])
                dve.tensor_scalar(qrow[:, j % 2, :], qrow[:, j % 2, :], FP8_MAX, -FP8_MAX, ALU.min, ALU.max)\
                    .then_inc(s_q, 1)

            def residual2(b, g, odd):
                t, h = divmod(g, HALVES)
                dve.wait_ge(s_down, NG * b + g + 1)
                at = xs[odd][:, t, h * 512:(h + 1) * 512]
                dve.scalar_tensor_tensor(out=at, in0=ps_down[g % 2][:, :], scalar=fac[:, 4:5], in1=at,
                                         op0=ALU.mult, op1=ALU.add).then_inc(s_out, 1)

            for t in range(TT):
                ln1_stats(0, t, 0)
            norm1(0)
            centre(0, 0)
            centre(0, 1)
            for t in range(TT):
                maxima(0, t)
            for t in range(TT):
                normalise(0, t)
            residual1(0, 0, 0)
            residual1(0, 1, 0)
            x1_stats(0, 0, 0)
            residual1(0, 2, 0)
            norm2(0, 0)
            residual1(0, 3, 0)
            x1_stats(0, 1, 0)
            row_exponent(0, 0)
            norm2(0, 1)
            row_add(0, 0)
            row_exponent(0, 1)
            row_subtract(0, 0)
            row_add(0, 1)
            row_clip(0)
            row_subtract(0, 1)
            row_exponent(0, 2)
            row_clip(1)
            row_add(0, 2)
            row_exponent(0, 3)
            row_subtract(0, 2)
            row_add(0, 3)
            row_clip(2)
            row_subtract(0, 3)
            row_clip(3)

            def row(b, odd, following):
                fence()
                a = b + 1
                for p in range(PAIRS):
                    if following:
                        if p == 0:
                            ln1_stats(a, 0, 1 - odd)
                        if p == 4:
                            for t in range(TT):
                                maxima(a, t)
                        if p == 6:
                            for t in range(TT):
                                for h in range(HALVES):
                                    residual1(a, t * HALVES + h, 1 - odd)
                                x1_stats(a, t, 1 - odd)
                    hidden_product(b, p)
                    if following and p == 2:
                        norm1(a)
                    if p >= 1:
                        hidden_subtract(b, p - 1)
                    hidden_exponent(b, p)
                    if p >= 1:
                        hidden_clip(p - 1)
                    hidden_range(p)
                    if following:
                        if p == 1:
                            ln1_stats(a, 1, 1 - odd)
                        if p in (2, 3):
                            centre(a, p - 2)
                        if p == 6:
                            for t in range(TT):
                                norm2(a, t)
                        if p == 4:
                            for t in range(TT):
                                normalise(a, t)
                        if p == 8:
                            row_exponent(a, 0)
                        if p == 9:
                            row_add(a, 0)
                        if p == 10:
                            row_exponent(a, 1)
                    hidden_add(p)
                    if following and p == 9:
                        row_subtract(a, 0)
                if following:
                    row_clip(0)
                hidden_subtract(b, PAIRS - 1)
                hidden_clip(PAIRS - 1)
                if following:
                    row_add(a, 1)
                    row_subtract(a, 1)
                    row_exponent(a, 2)
                    row_clip(1)
                residual2(b, 0, odd)
                if following:
                    row_add(a, 2)
                    row_exponent(a, 3)
                    row_subtract(a, 2)
                residual2(b, 1, odd)
                if following:
                    row_add(a, 3)
                    row_clip(2)
                    row_subtract(a, 3)
                    row_clip(3)
                residual2(b, 2, odd)
                residual2(b, 3, odd)

            row(0, 0, True)
            with dve.Fori(1, BATCH - 2, 2) as b:
                row(b, 1, True)
                row(b + 1, 0, True)
            row(BATCH - 1, 1, False)


def kernel(x, ctx_4096, g_xattn, g_ffn, L0_ffn_gate_w, L0_ffn_up_w, L0_ffn_down_w, L0_ffn_gate_w_scale,
           L0_ffn_up_w_scale, L0_ffn_down_w_scale, L0_ffn_gate_in_scale, L0_ffn_up_in_scale, L0_ffn_down_in_scale):
    import numpy as np
    import concourse.bacc as bacc
    from concourse.bass_utils import run_bass_kernel_spmd

    def up_pairs(w):
        w = np.asarray(w)
        main = w[:FULL * 256].reshape(FULL, 256, KD, P).transpose(3, 0, 2, 1)
        tail = w[FULL * 256:].reshape(TAIL, KD, P).transpose(2, 1, 0)
        return np.ascontiguousarray(main), np.ascontiguousarray(tail)

    gate_main, gate_tail = up_pairs(L0_ffn_gate_w)
    up_main, up_tail = up_pairs(L0_ffn_up_w)
    down = np.asarray(L0_ffn_down_w)
    down_main = np.ascontiguousarray(down[:, :(KI - 1) * P].reshape(DIM, KI - 1, P).transpose(2, 1, 0))
    down_tail = np.ascontiguousarray(down[:, (KI - 1) * P:].transpose(1, 0))
    x = np.ascontiguousarray(np.asarray(x))
    x_t = np.ascontiguousarray(x.reshape(BATCH, SEQ, KD, P).transpose(0, 3, 2, 1))
    ctx = np.ascontiguousarray(np.asarray(ctx_4096))
    ctx_t = np.ascontiguousarray(ctx.reshape(BATCH, SEQ, KD, P).transpose(0, 3, 2, 1))
    scalars = np.concatenate([np.asarray(s).reshape(1, 1) for s in (
        g_xattn, g_ffn, L0_ffn_gate_w_scale, L0_ffn_up_w_scale, L0_ffn_down_w_scale,
        L0_ffn_gate_in_scale, L0_ffn_up_in_scale, L0_ffn_down_in_scale)], axis=1)

    nc = bacc.Bacc("TRN2", target_bir_lowering=False, num_devices=1)
    arrays, args = {}, []
    for name, a in (("x", x), ("x_t", x_t), ("ctx", ctx), ("ctx_t", ctx_t), ("scalars", scalars),
                    ("gate_main", gate_main), ("gate_tail", gate_tail), ("up_main", up_main),
                    ("up_tail", up_tail), ("down_main", down_main), ("down_tail", down_tail)):
        arrays[name] = a
        args.append(nc.dram_tensor(name, a.shape, mybir.dt.from_np(a.dtype), kind="ExternalInput").ap())
    args.append(nc.dram_tensor("out", (BATCH, SEQ, DIM), mybir.dt.float32, kind="ExternalOutput").ap())
    gated_xattn_ffn(nc, *args)
    r = run_bass_kernel_spmd(nc, [arrays], core_ids=[0])
    return r.results[0]["out"]
```
